# Optimizing a Trainium2 kernel written in Bass

```python
import numpy as np
import jax
import jax.numpy as jnp

def _softmax(x, axis=-1):
    return jax.nn.softmax(x, axis=axis)

def _gelu(x):
    return jax.nn.gelu(x, approximate=True)

def _silu(x):
    return jax.nn.silu(x)

def _sigmoid(x):
    return jax.nn.sigmoid(x)

def _layernorm(x, axis=-1, eps=1e-05):
    m = jnp.mean(x, axis=axis, keepdims=True)
    v = jnp.var(x, axis=axis, keepdims=True)
    return (x - m) / jnp.sqrt(v + eps)

def _scatter_add(tgt, idx, src, axis=0):
    return tgt.at[idx].add(src)

def _segment_sum(src, seg, n):
    return jax.ops.segment_sum(src, seg, n)
kernel_name = 'mk_xattn_ffn_d1_seqx_r8_db92a5'

def setup_inputs(seed: int=0):
    np.random.seed(seed)
    _w = jnp.asarray

    def _rec_inputs():
        import jax
        import jax.numpy as jnp
        _rk = jax.random.key(seed)
        x = -0.0005207 + 1.001 * jax.random.normal(jax.random.fold_in(_rk, 1), (8, 128, 512), jnp.float32)
        _lenS = 128 - jax.random.randint(jax.random.fold_in(_rk, 7), (8,), 0, max(1, 128 // 4) + 1, jnp.int32)
        _lenS2 = 128 - jax.random.randint(jax.random.fold_in(_rk, 8), (8,), 0, max(1, 128 // 4) + 1, jnp.int32)
        _ctx_4096P = jax.random.normal(jax.random.fold_in(_rk, 11), (8, 16, 512), jnp.float32)
        _ctx_4096c = jax.random.dirichlet(jax.random.fold_in(_rk, 511), 0.3 * jnp.ones((16,), jnp.float32), (8, 128))
        _ctx_4096t = jnp.einsum('bsk,bkd->bsd', _ctx_4096c, _ctx_4096P)
        _ctx_4096t = _ctx_4096t * jax.lax.rsqrt(jnp.mean(jnp.square(_ctx_4096t)) + 1e-12) * 0.953939
        ctx_4096 = -0.00010331 + 0.999899 * (_ctx_4096t + 0.3 * jax.random.normal(jax.random.fold_in(_rk, 611), (8, 128, 512), jnp.float32))
        return (x, ctx_4096)
    x, ctx_4096 = _rec_inputs()

    def _L0_xattn_setup():
        import jax, jax.numpy as jnp
        import numpy as np
        import math
        HIDDEN = 512
        N_HEADS = 32
        HEAD_DIM = 128
        N_KV_HEADS = 4
        N_GROUPS = N_HEADS // N_KV_HEADS
        key = jax.random.key(seed)
        ks = jax.random.split(key, 6)
        B, NL, S = (8, 64, 512)
        latents = jax.random.normal(ks[0], (B, NL, HIDDEN), dtype=jnp.float32)
        context = jax.random.normal(ks[1], (B, S, HIDDEN), dtype=jnp.float32)
        scale = 1.0 / math.sqrt(HIDDEN)
        Wq = jax.random.normal(ks[2], (HIDDEN, N_HEADS * HEAD_DIM), dtype=jnp.float32) * scale
        Wk = jax.random.normal(ks[3], (HIDDEN, N_KV_HEADS * HEAD_DIM), dtype=jnp.float32) * scale
        Wv = jax.random.normal(ks[4], (HIDDEN, N_KV_HEADS * HEAD_DIM), dtype=jnp.float32) * scale
        Wo = jax.random.normal(ks[5], (N_HEADS * HEAD_DIM, HIDDEN), dtype=jnp.float32) * scale
        return {'latents': latents, 'context': context, 'Wq': Wq, 'Wk': Wk, 'Wv': Wv, 'Wo': Wo}
    _L0_xattn_all = _L0_xattn_setup()
    _L0_xattn_in = {k: v for k, v in _L0_xattn_all.items() if k in ('Wq', 'Wk', 'Wv', 'Wo')}
    del _L0_xattn_all

    def _L0_ffn_setup():
        import jax, jax.numpy as jnp
        import numpy as np

        @jax.custom_vjp
        def ste_sign(w):
            return jnp.sign(w)

        def _ste_fwd(w):
            return (jnp.sign(w), w)

        def _ste_bwd(w, g):
            mask = ((w > -1) & (w < 1)).astype(g.dtype)
            return (g * mask,)
        ste_sign.defvjp(_ste_fwd, _ste_bwd)
        key = jax.random.key(seed)
        k = jax.random.split(key, 6)
        B, S, H, O, E = (4, 256, 512, 512, 8)
        return {'x': jax.random.normal(k[0], (B, S, H), dtype=jnp.float32), 'weight': jax.random.normal(k[1], (O, H), dtype=jnp.float32) * 0.02, 'bias': jax.random.normal(k[2], (O,), dtype=jnp.float32) * 0.02, 'gate_w': jax.random.normal(k[3], (E, H), dtype=jnp.float32) * 0.02, 'in_channel_scale': jax.random.normal(k[4], (E, H), dtype=jnp.float32), 'out_channel_scale': jax.random.normal(k[5], (E, O), dtype=jnp.float32)}
    _L0_ffn_all = _L0_ffn_setup()
    _L0_ffn_in = {k: v for k, v in _L0_ffn_all.items() if k in ('weight', 'bias', 'gate_w', 'in_channel_scale', 'out_channel_scale')}
    del _L0_ffn_all
    return {'x': x, 'ctx_4096': ctx_4096, 'L0_xattn_Wq': _L0_xattn_in['Wq'], 'L0_xattn_Wk': _L0_xattn_in['Wk'], 'L0_xattn_Wv': _L0_xattn_in['Wv'], 'L0_xattn_Wo': _L0_xattn_in['Wo'], 'L0_ffn_weight': _L0_ffn_in['weight'], 'L0_ffn_bias': _L0_ffn_in['bias'], 'L0_ffn_gate_w': _L0_ffn_in['gate_w'], 'L0_ffn_in_channel_scale': _L0_ffn_in['in_channel_scale'], 'L0_ffn_out_channel_scale': _L0_ffn_in['out_channel_scale']}

def reference(x, ctx_4096, L0_xattn_Wq, L0_xattn_Wk, L0_xattn_Wv, L0_xattn_Wo, L0_ffn_weight, L0_ffn_bias, L0_ffn_gate_w, L0_ffn_in_channel_scale, L0_ffn_out_channel_scale):
    import jax
    import jax.numpy as jnp

    def _L0_xattn_ref(latents, context, Wq, Wk, Wv, Wo):
        import jax, jax.numpy as jnp
        import numpy as np
        import math
        HIDDEN = 512
        N_HEADS = 32
        HEAD_DIM = 128
        N_KV_HEADS = 4
        N_GROUPS = N_HEADS // N_KV_HEADS
        b, q_len, _ = latents.shape
        kv_len = q_len + context.shape[1]
        hidden_states = jnp.concatenate([context, latents], axis=1)
        q = (latents @ Wq).reshape(b, q_len, N_KV_HEADS, N_GROUPS, HEAD_DIM)
        k = (hidden_states @ Wk).reshape(b, kv_len, N_KV_HEADS, HEAD_DIM)
        v = (hidden_states @ Wv).reshape(b, kv_len, N_KV_HEADS, HEAD_DIM)
        scale = 1.0 / math.sqrt(HEAD_DIM)
        scores = jnp.einsum('bqhgd,bkhd->bhgqk', q, k) * scale
        attn = jax.nn.softmax(scores.astype(jnp.float32), axis=-1).astype(q.dtype)
        out = jnp.einsum('bhgqk,bkhd->bqhgd', attn, v)
        out = out.reshape(b, q_len, N_HEADS * HEAD_DIM)
        return out @ Wo

    def _L0_ffn_ref(x, weight, bias, gate_w, in_channel_scale, out_channel_scale):
        import jax, jax.numpy as jnp
        import numpy as np

        @jax.custom_vjp
        def ste_sign(w):
            return jnp.sign(w)

        def _ste_fwd(w):
            return (jnp.sign(w), w)

        def _ste_bwd(w, g):
            mask = ((w > -1) & (w < 1)).astype(g.dtype)
            return (g * mask,)
        ste_sign.defvjp(_ste_fwd, _ste_bwd)
        B, S, H = x.shape
        xf = x.reshape(-1, H)
        router_logits = xf @ gate_w.T
        routing = jax.nn.softmax(router_logits.astype(jnp.float32), axis=1).astype(x.dtype)
        in_scale = routing @ in_channel_scale
        out_scale = routing @ out_channel_scale
        wb = ste_sign(weight)
        out = xf * in_scale @ wb.T * out_scale + bias
        return out.reshape(B, S, -1)
    x = x + _L0_xattn_ref(_layernorm(x, axis=-1), ctx_4096, L0_xattn_Wq, L0_xattn_Wk, L0_xattn_Wv, L0_xattn_Wo)
    x = x + _L0_ffn_ref(_layernorm(x, axis=-1), L0_ffn_weight, L0_ffn_bias, L0_ffn_gate_w, L0_ffn_in_channel_scale, L0_ffn_out_channel_scale)
    return x

_drawn_inputs = setup_inputs


def setup_inputs(seed=0):
    import zlib

    import numpy as np

    out = dict(_drawn_inputs(seed))
    spreads = {}
    factors = {'L0_ffn_bias': 8.0}
    for name, (base, spread) in spreads.items():
        noise = np.random.default_rng([zlib.crc32(name.encode()), seed]).standard_normal(out[name].shape)
        drawn = base * np.exp(spread * noise) if base else spread * noise
        out[name] = jnp.asarray(drawn.astype(out[name].dtype))
    for name, factor in factors.items():
        out[name] = (out[name] * factor).astype(out[name].dtype)
    return out
```

```python
import concourse.bass as bass
from concourse import mybir
from contextlib import ExitStack

HI, LO = 0, 1
TERMS = ((HI, HI), (HI, LO), (LO, HI))


def xattn_ffn(nc, x, ctx, wq, wk, wv, wo, ffn_w, ffn_b, gate_w, in_cs, out_cs, out):
    fp32 = mybir.dt.float32
    f32r = mybir.dt.float32r
    ALU = mybir.AluOpType
    ACT = mybir.ActivationFunctionType
    AX = mybir.AxisListType

    P = 128
    B, T, D = x.shape
    HC = D // P
    HEADS = wq.shape[1] // P
    G = wk.shape[1] // P
    QH = 4
    QUADS = HEADS // G // QH
    KEYS = 2 * T
    KC = KEYS // P
    E = gate_w.shape[0]
    HALF = 4
    NHALF = B // HALF
    UNITS = NHALF * QH
    PRE_UNITS = 2 * B + 2 * G * NHALF
    SCALE = float(P) ** -0.5
    EPS = 1e-5

    es = ExitStack()
    with es:
        def sb(stack, name, shape, dt=fp32):
            return stack.enter_context(nc.sbuf_tensor(name, shape, dt))

        def sem(name):
            return es.enter_context(nc.semaphore(name))

        k_park = nc.dram_tensor("k_park", (G, P, B, 2, KEYS), fp32).ap()
        v_park = nc.dram_tensor("v_park", (G, P, B, 2, KC, P), fp32).ap()

        xT = sb(es, "xT", [P, 2, HC, B * T], f32r)
        acc = sb(es, "acc", [P, B, D])
        wq_pair = sb(es, "wq_pair", [P, 2, HC, QH * P], f32r)
        raw_a = sb(es, "raw_a", [P, HC, D])
        raw_b = sb(es, "raw_b", [P, QH, D])
        ident = sb(es, "ident", [P, P])
        y = sb(es, "y", [P, 2, D])
        stats = sb(es, "stats", [P, 2, 6])
        mv = sb(es, "mv", [P, 2 * B, 2])
        vare = sb(es, "vare", [P, 2 * B])
        rstd0 = sb(es, "rstd0", [P, 2 * B])
        nwt = sb(es, "nwt", [P, 2 * B])
        nwt2 = sb(es, "nwt2", [P, 2 * B])
        nwt3 = sb(es, "nwt3", [P, 2 * B])
        rstd = sb(es, "rstd", [P, 2 * B])
        neg_half = sb(es, "neg_half", [P, 1])
        nmax = sb(es, "nmax", [P, 2, 2])
        esum = sb(es, "esum", [P, 2, 2])
        rsum = sb(es, "rsum", [P, 2, 2])
        bias_b = sb(es, "bias_b", [P, D])
        gate_sb = sb(es, "gate_sb", [E, D])
        ics = sb(es, "ics", [E, D])
        ocs = sb(es, "ocs", [E, D])
        gateT = sb(es, "gateT", [P, HC, E])
        neg = sb(es, "neg", [P, D])
        with ExitStack() as pre:
            cT = sb(pre, "cT", [P, 2, HC, B * T], f32r)
            wv_pair = sb(pre, "wv_pair", [P, 2, HC, D], f32r)
            craw = sb(pre, "craw", [P, B, D])
            wk_pair = sb(pre, "wk_pair", [P, 2, HC, D], f32r)
            v_stage = sb(pre, "v_stage", [P, 2, G, 2, KC, P], f32r)
            k_stage = sb(pre, "k_stage", [P, 2, HALF, 2, KC, P], f32r)
        with ExitStack() as att:
            qT = sb(att, "qT", [P, 2, QH, B * T], f32r)
            wo_pair = sb(att, "wo_pair", [P, 2, QH, D], f32r)
            kg = sb(att, "kg", [P, B, 2, KEYS], f32r)
            vg = sb(att, "vg", [P, B, 2, KC, P], f32r)
            prob = sb(att, "prob", [P, 2, 2, KEYS])
            pT = sb(att, "pT", [P, 2, KC, QH, T], f32r)
            oT = sb(att, "oT", [P, 2, QH, T], f32r)
        with ExitStack() as ffn:
            sgnT = sb(ffn, "sgnT", [P, HC, D], f32r)
            yT = sb(ffn, "yT", [P, 2, HC, T])
            z_pair = sb(ffn, "z_pair", [P, 2, 2, HC, T], f32r)
            z = sb(ffn, "z", [P, HC, T])
            oscale = sb(ffn, "oscale", [P, 2, D])
            gmax = sb(ffn, "gmax", [P, 1])
            gexp = sb(ffn, "gexp", [P, E])
            gsum = sb(ffn, "gsum", [P, 1])
            grec = sb(ffn, "grec", [P, 1])
            route = sb(ffn, "route", [P, E])
            routeT = sb(ffn, "routeT", [E, T])

        bank = [es.enter_context(nc.psum_tensor(f"bank{i}", [P, 512], fp32)) for i in range(8)]
        s_bank, t_bank, proj_bank = bank[0:2], bank[2:4], bank[6:8]
        av_bank, wo_bank = bank[4], bank[5]
        ffn_bank = [s_bank[1], proj_bank[1]]

        x_in = [sem(f"x_in{b}") for b in range(B)]
        c_in = [sem(f"c_in{b}") for b in range(B)]
        wv_in, wk_in, wq_in, wo_in, small_in, ffn_in = (
            sem(n) for n in ("wv_in", "wk_in", "wq_in", "wo_in", "small_in", "ffn_in"))
        k_in = [sem(f"k_in{b}") for b in range(B)]
        v_in = [sem(f"v_in{b}") for b in range(B)]
        v_parked = [sem(f"v_parked{i}") for i in range(2)]
        k_parked = [sem(f"k_parked{i}") for i in range(2)]
        out_stored = sem("out_stored")
        zeroed, const_ready = sem("zeroed"), sem("const_ready")
        wv_hi, wv_lo, wk_hi, wk_lo, wq_hi, wq_lo, wo_hi, wo_lo = (
            sem(n) for n in ("wv_hi", "wv_lo", "wk_hi", "wk_lo", "wq_hi", "wq_lo", "wo_hi", "wo_lo"))
        stats_ready, mv_ready, rstd_ready, rstd_step, y_ready = (
            sem(n) for n in ("stats_ready", "mv_ready", "rstd_ready", "rstd_step", "y_ready"))
        xt_ready, xt_hi, xt_lo, ct_ready, ct_hi, ct_lo = (
            sem(n) for n in ("xt_ready", "xt_hi", "xt_lo", "ct_ready", "ct_hi", "ct_lo"))
        proj_ready, proj_hi, proj_lo = sem("proj_ready"), sem("proj_hi"), sem("proj_lo")
        s_ready, max_ready, exp_ready, rsum_ready, prob_ready, pt_ready, pt_hi, pt_lo = (
            [sem(f"{n}{p}") for p in range(2)]
            for n in ("s_ready", "max_ready", "exp_ready", "rsum_ready", "prob_ready", "pt_ready",
                      "pt_hi", "pt_lo"))
        av_ready, o_hi, o_lo, wo_ready, acc_ready = (
            sem(n) for n in ("av_ready", "o_hi", "o_lo", "wo_ready", "acc_ready"))
        sgn_step, sgn_ready, sgnt_ready, sgnt_copied, gatet_ready, gatet_copied = (
            sem(n) for n in ("sgn_step", "sgn_ready", "sgnt_ready", "sgnt_copied", "gatet_ready",
                             "gatet_copied"))
        yt_ready, yt_copied, logit_ready, gmax_ready, gexp_ready, grec_ready, route_ready = (
            sem(n) for n in ("yt_ready", "yt_copied", "logit_ready", "gmax_ready", "gexp_ready",
                             "grec_ready", "route_ready"))
        routet_ready, routet_copied, iscale_ready, oscale_ready, oscale_copied = (
            sem(n) for n in ("routet_ready", "routet_copied", "iscale_ready", "oscale_ready",
                             "oscale_copied"))
        z_ready, z_hi, z_lo, ffn_ready, scaled_ready, bias_added, out_ready = (
            sem(n) for n in ("z_ready", "z_hi", "z_lo", "ffn_ready", "scaled_ready", "bias_added",
                             "out_ready"))

        block = es.enter_context(nc.Block())

        def count(g, per_quad, qd, k):
            return g * (QUADS * per_quad) + (per_quad * qd + k)

        def steps(g, qd, k):
            return g * (QUADS * B) + (B * qd + k + 1)

        def open_loop(engine, *semaphores):
            for s in semaphores:
                engine.sem_inc(s, 1)

        @block.sync
        def _(sp):
            wq_v = wq.rearrange("(c p) n -> p c n", p=P)
            wo_v = wo.rearrange("(h p) n -> p h n", p=P)

            def words(pair):
                return pair.bitcast(fp32)

            def load_x(b):
                sp.dma_start(acc[:, b, :], x[b]).then_inc(x_in[b], 16)

            def load_c(b):
                sp.dma_start(craw[:, b, :], ctx[b]).then_inc(c_in[b], 16)

            def load_wq(g, quad):
                cols = bass.ds(g * (QUADS * QH * P) + quad * QH * P, QH * P)
                sp.dma_start(raw_a[:, :, :], wq_v[:, :, cols]).then_inc(wq_in, 16)

            def load_wo(g, quad):
                heads = bass.ds(g * (QUADS * QH) + quad * QH, QH)
                sp.dma_start(raw_b[:, :, :], wo_v[:, heads, :]).then_inc(wo_in, 16)

            def load_kv(g, b):
                sp.dma_start(words(kg[:, b, :, :]), k_park[bass.ds(g, 1), :, b, :, :].rearrange(
                    "a p s k -> p (a s) k")).then_inc(k_in[b], 16)
                sp.dma_start(words(vg[:, b, :, :, :]), v_park[bass.ds(g, 1), :, b, :, :, :].rearrange(
                    "a p s c k -> p (a s) c k")).then_inc(v_in[b], 16)

            load_x(0)
            sp.dma_start(raw_a[:, :, :], wv.rearrange("(c p) n -> p c n", p=P)).then_inc(wv_in, 16)
            load_c(0)
            load_x(1)
            load_c(1)
            sp.dma_start(raw_b[:, :, :], wk.rearrange("(c p) n -> p c n", p=P)).then_inc(wk_in, 16)
            for b in range(2, B):
                load_x(b)
                load_c(b)
            sp.dma_start(gate_sb[:, :], gate_w).then_inc(small_in, 16)
            sp.dma_start(ics[:, :], in_cs).then_inc(small_in, 16)
            sp.dma_start(ocs[:, :], out_cs).then_inc(small_in, 16)
            sp.dma_start(bias_b[:, :], ffn_b.rearrange("(a n) -> a n", a=1).broadcast_to((P, D))
                         ).then_inc(small_in, 16)
            sp.wait_ge(wv_lo, HC)
            load_wq(0, 0)
            sp.wait_ge(wk_lo, HC)
            load_wo(0, 0)
            for b in range(B):
                sp.wait_ge(proj_lo, 2 * b + 2)
                sp.dma_start(v_park[:, :, b].rearrange("g p s c k -> p g (s c k)"),
                             words(v_stage[:, b % 2]).rearrange("p g s c k -> p g (s c k)")
                             ).then_inc(v_parked[b % 2], 16)
            for u in range(G * NHALF):
                g, half = divmod(u, NHALF)
                sp.wait_ge(proj_lo, 2 * B + 2 * u + 2)
                sp.dma_start(k_park[g, :, half * HALF:(half + 1) * HALF].rearrange(
                    "p b s k -> p (b s k)"), words(k_stage[:, u % 2]).rearrange("p b s c k -> p (b s c k)")
                    ).then_inc(k_parked[u % 2], 16)
            for i in range(2):
                sp.wait_ge(v_parked[i], 16 * (B // 2))
                sp.wait_ge(k_parked[i], 16 * (G * NHALF // 2))
            sp.wait_ge(proj_ready, PRE_UNITS)
            for b in range(B):
                load_kv(0, b)

            def group(g, last):
                for qd in range(QUADS):
                    if last and qd == QUADS - 1:
                        sp.wait_ge(wq_lo, count(g, HC, qd, HC))
                        sp.dma_start(raw_a[:, :, :], ffn_w.rearrange("(c p) n -> p c n", p=P)
                                     ).then_inc(ffn_in, 16)
                        break
                    sp.wait_ge(wq_lo, count(g, HC, qd, HC))
                    load_wq(g, qd + 1)
                    sp.wait_ge(wo_lo, count(g, QH, qd, QH))
                    load_wo(g, qd + 1)
                if not last:
                    qd = QUADS - 1
                    for b in range(B):
                        for p in range(2):
                            sp.wait_ge(s_ready[p], steps(g, qd, b + 1))
                        sp.wait_ge(av_ready, steps(g, qd, b + 1))
                        load_kv(g + 1, b)

            with sp.Fori(0, G - 1) as g:
                group(g, False)
            group(G - 1, True)

            for b in range(B):
                sp.wait_ge(out_ready, b + 1)
                sp.dma_start(out[b], acc[:, b, :]).then_inc(out_stored, 16)
            sp.wait_ge(out_stored, 16 * B)

        @block.gpsimd
        def _(pool):
            open_loop(pool, *prob_ready)
            pool.memset(ident[:, :], 0.0).then_inc(zeroed, 1)
            pool.memset(neg_half[:, :], -0.5).then_inc(const_ready, 1)
            pool.wait_ge(zeroed, 1)
            pool.affine_select(out=ident[:, :], in_=ident[:, :], compare_op=ALU.not_equal, fill=1.0,
                               base=0, pattern=[[-1, P]], channel_multiplier=1
                               ).then_inc(const_ready, 1)

            def split_lo(pair, raw, c, hi_sem, hi_count, lo_sem):
                pool.wait_ge(hi_sem, hi_count)
                nc.gpsimd.tensor_tensor(pair[:, LO, c, :], raw[:, c, :], pair[:, HI, c, :],
                                        ALU.subtract).then_inc(lo_sem, 1)

            def make_rstd(i):
                step = 4 * i
                col = slice(i, i + 1)
                pool.wait_ge(mv_ready, i + 1)
                nc.gpsimd.tensor_scalar(vare[:, col], mv[:, i, 1:2], EPS, None, ALU.add
                                        ).then_inc(rstd_step, 1)
                pool.wait_ge(rstd_step, step + 1)
                nc.gpsimd.tensor_tensor(rstd0[:, col], vare[:, col], neg_half[:, :], ALU.pow
                                        ).then_inc(rstd_step, 1)
                pool.wait_ge(rstd_step, step + 2)
                nc.gpsimd.tensor_tensor(nwt[:, col], rstd0[:, col], rstd0[:, col], ALU.mult
                                        ).then_inc(rstd_step, 1)
                pool.wait_ge(rstd_step, step + 3)
                nc.gpsimd.tensor_tensor(nwt2[:, col], nwt[:, col], vare[:, col], ALU.mult
                                        ).then_inc(rstd_step, 1)
                pool.wait_ge(rstd_step, step + 4)
                nc.gpsimd.tensor_scalar(nwt3[:, col], nwt2[:, col], -0.5, 1.5, ALU.mult, ALU.add
                                        ).then_inc(rstd_ready, 1)
                pool.wait_ge(rstd_ready, 2 * i + 1)
                nc.gpsimd.tensor_tensor(rstd[:, col], rstd0[:, col], nwt3[:, col], ALU.mult
                                        ).then_inc(rstd_ready, 1)

            pool.wait_ge(const_ready, 2)
            make_rstd(0)
            for c in range(HC):
                split_lo(wv_pair, raw_a, c, wv_hi, c + 1, wv_lo)
            make_rstd(1)
            for c in range(HC):
                split_lo(wk_pair, raw_b, c, wk_hi, c + 1, wk_lo)
            for b in range(2, B):
                make_rstd(b)
            for c in range(HC):
                split_lo(wq_pair, raw_a, c, wq_hi, c + 1, wq_lo)

            def normalise(g, qd, t, p):
                pool.wait_ge(exp_ready[p], steps(g, qd, t + 1))
                pool.wait_ge(rsum_ready[p], steps(g, qd, t + 1))
                nc.gpsimd.tensor_tensor(prob[:, p], prob[:, p],
                                        rsum[:, p].unsqueeze(2).to_broadcast([P, 2, KEYS]),
                                        ALU.mult).then_inc(prob_ready[p], 1)

            def group(g, last):
                for qd in range(QUADS):
                    for h in range(QH):
                        split_lo(wo_pair, raw_b, h, wo_hi, count(g, QH, qd, h + 1), wo_lo)
                    for p in range(2):
                        normalise(g, qd, 0, p)
                    for t in range(B):
                        if t + 1 < B:
                            for p in range(2):
                                normalise(g, qd, t + 1, p)
                        if 1 <= t <= HC and not (last and qd == QUADS - 1):
                            split_lo(wq_pair, raw_a, t - 1, wq_hi, count(g, HC, qd, HC + t), wq_lo)

            with pool.Fori(0, G - 1) as g:
                group(g, False)
            group(G - 1, True)

            pool.wait_ge(small_in, 64)
            make_rstd(B)
            make_rstd(B + 1)
            for i in range(B + 2):
                if i + 2 < B:
                    make_rstd(B + i + 2)
                if 0 <= i - 1 < B:
                    b = i - 1
                    pool.wait_ge(y_ready, B + b + 1)
                    nc.gpsimd.tensor_tensor(acc[:, b], acc[:, b], bias_b[:, :], ALU.add
                                            ).then_inc(bias_added, 1)
                if i - 2 >= 0:
                    b = i - 2
                    pool.wait_ge(scaled_ready, b + 1)
                    pool.wait_ge(bias_added, b + 1)
                    nc.gpsimd.tensor_tensor(acc[:, b], acc[:, b], oscale[:, b % 2], ALU.add
                                            ).then_inc(out_ready, 1)

        @block.scalar
        def _(act):
            open_loop(act, *exp_ready, *pt_hi, o_hi)

            def copy(dst, src):
                return nc.scalar.activation(dst, src, ACT.Copy)

            def split_hi(pair, raw, c, sem_):
                copy(pair[:, HI, c, :], raw[:, c, :]).then_inc(sem_, 1)

            def xt_half(b):
                act.wait_ge(xt_ready, b + 1)
                copy(xT[:, HI, :, b * T:(b + 1) * T],
                     t_bank[0][:, :].rearrange("p (c t) -> p c t", c=HC)).then_inc(xt_hi, 1)

            def ct_half(b):
                act.wait_ge(ct_ready, b + 1)
                copy(cT[:, HI, :, b * T:(b + 1) * T],
                     t_bank[1][:, :].rearrange("p (c t) -> p c t", c=HC)).then_inc(ct_hi, 1)

            act.wait_ge(wv_in, 16)
            for c in range(HC):
                split_hi(wv_pair, raw_a, c, wv_hi)
            xt_half(0)
            ct_half(0)
            for b in range(B):
                if b == 0:
                    act.wait_ge(wk_in, 16)
                    for c in range(HC):
                        split_hi(wk_pair, raw_b, c, wk_hi)
                if b + 1 < B:
                    xt_half(b + 1)
                    ct_half(b + 1)
                if b >= 2:
                    act.wait_ge(v_parked[b % 2], 16 * (b // 2))
                for kc in range(KC):
                    n = 2 * b + kc
                    act.wait_ge(proj_ready, n + 1)
                    copy(v_stage[:, b % 2, :, HI, kc, :],
                         proj_bank[n % 2][:, :].rearrange("p (g d) -> p g d", g=G)
                         ).then_inc(proj_hi, 1)
            act.wait_ge(wq_in, 16)
            for c in range(HC):
                split_hi(wq_pair, raw_a, c, wq_hi)
            for u in range(G * NHALF):
                if u >= 2:
                    act.wait_ge(k_parked[u % 2], 16 * (u // 2))
                for kc in range(KC):
                    n = 2 * B + 2 * u + kc
                    act.wait_ge(proj_ready, n + 1)
                    copy(k_stage[:, u % 2, :, HI, kc, :],
                         proj_bank[n % 2][:, :].rearrange("p (b t) -> p b t", b=HALF)
                         ).then_inc(proj_hi, 1)
            for i in range(2):
                act.wait_ge(v_parked[i], 16 * (B // 2))

            def q_half(g, qd, u):
                half, h = divmod(u, QH)
                act.wait_ge(proj_ready, count(g, UNITS, qd, PRE_UNITS + u + 1))
                act.wait_ge(s_ready[h // 2], steps(g, qd, 0))
                nc.scalar.activation(qT[:, HI, h, half * 512:(half + 1) * 512],
                                     proj_bank[u % 2][:, :], ACT.Copy, scale=SCALE
                                     ).then_inc(proj_hi, 1)

            def exps(g, qd, t, p):
                act.wait_ge(max_ready[p], steps(g, qd, t + 1))
                act.wait_ge(pt_ready[p], steps(g, qd, t))
                for j in range(2):
                    ins = nc.scalar.activation(prob[:, p, j], s_bank[p][:, j * KEYS:(j + 1) * KEYS],
                                               ACT.Exp, bias=nmax[:, p, j:j + 1],
                                               accum_out=esum[:, p, j:j + 1])
                ins.then_inc(exp_ready[p], 1)

            def pt_half(g, qd, t, p):
                act.wait_ge(pt_ready[p], steps(g, qd, t + 1))
                act.wait_ge(av_ready, steps(g, qd, t))
                copy(pT[:, HI, :, 2 * p:2 * p + 2, :],
                     t_bank[p][:, :].rearrange("p (c h t) -> p c h t", c=KC, h=2)
                     ).then_inc(pt_hi[p], 1)

            def group(g, last):
                for qd in range(QUADS):
                    for u in range(QH):
                        q_half(g, qd, u)
                        if u == 1:
                            act.wait_ge(wo_in, 16 * (count(g, 1, qd, 1)))
                            act.wait_ge(wo_ready, steps(g, qd, 0))
                            for h in range(QH):
                                split_hi(wo_pair, raw_b, h, wo_hi)
                    exps(g, qd, 0, 0)
                    exps(g, qd, 0, 1)
                    for u in range(QH, UNITS):
                        q_half(g, qd, u)
                    for t in range(B):
                        for p in range(2):
                            pt_half(g, qd, t, p)
                            if t + 1 < B:
                                exps(g, qd, t + 1, p)
                        if 1 <= t <= HC and not (last and qd == QUADS - 1):
                            if t == 1:
                                act.wait_ge(wq_in, 16 * count(g, 1, qd, 2))
                            split_hi(wq_pair, raw_a, t - 1, wq_hi)
                        act.wait_ge(av_ready, steps(g, qd, t + 1))
                        act.wait_ge(wo_ready, steps(g, qd, t))
                        copy(oT[:, HI].rearrange("p h t -> p (h t)"), av_bank[:, :]
                             ).then_inc(o_hi, 1)

            with act.Fori(0, G - 1) as g:
                group(g, False)
            group(G - 1, True)

            act.wait_ge(gatet_ready, 1)
            copy(gateT[:, :, :], bank[0][:, 0:HC * E].rearrange("p (c e) -> p c e", c=HC)
                 ).then_inc(gatet_copied, 1)
            for c in range(HC):
                act.wait_ge(sgnt_ready, c + 1)
                copy(sgnT[:, c, :], proj_bank[c % 2][:, :]).then_inc(sgnt_copied, 1)
            for i in range(B + 1):
                if i < B:
                    act.wait_ge(yt_ready, i + 1)
                    if i >= 2:
                        act.wait_ge(z_ready, i - 1)
                        act.wait_ge(logit_ready, i - 1)
                    copy(yT[:, i % 2], t_bank[i % 2][:, :].rearrange("p (c t) -> p c t", c=HC)
                         ).then_inc(yt_copied, 1)
                if i >= 1:
                    b = i - 1
                    act.wait_ge(routet_ready, b + 1)
                    act.wait_ge(oscale_ready, b)
                    copy(routeT[:, :], proj_bank[0][0:E, 0:T]).then_inc(routet_copied, 1)
                    act.wait_ge(oscale_ready, b + 1)
                    if b >= 2:
                        act.wait_ge(out_ready, b - 1)
                    copy(oscale[:, b % 2], wo_bank[:, :]).then_inc(oscale_copied, 1)
                    act.wait_ge(z_ready, b + 1)
                    if b >= 2:
                        act.wait_ge(ffn_ready, b - 1)
                    copy(z_pair[:, b % 2, HI], z[:, :, :]).then_inc(z_hi, 1)
                if i < B:
                    act.wait_ge(gmax_ready, i + 1)
                    nc.scalar.activation(gexp[:, :], s_bank[0][:, 0:E], ACT.Exp, bias=gmax[:, :],
                                         accum_out=gsum[:, :]).then_inc(gexp_ready, 1)

        @block.vector
        def _(dve):
            open_loop(dve, *max_ready, *rsum_ready, *pt_lo, o_lo, acc_ready)

            def subtract(dst, a, b):
                return nc.vector.tensor_tensor(dst, a, b, ALU.subtract)

            def layer_stats(i, b):
                nc.vector.bn_stats(stats[:, i % 2], acc[:, b, :]).then_inc(stats_ready, 1)
                dve.wait_ge(stats_ready, i + 1)
                nc.vector.bn_aggr(mv[:, i], stats[:, i % 2]).then_inc(mv_ready, 1)

            def layer_norm(i, b):
                dve.wait_ge(rstd_ready, 2 * i + 2)
                nc.vector.tensor_scalar(y[:, i % 2], acc[:, b, :], mv[:, i, 0:1], rstd[:, i:i + 1],
                                        ALU.subtract, ALU.mult).then_inc(y_ready, 1)

            def xt_rest(b):
                dve.wait_ge(xt_hi, b + 1)
                part = xT[:, :, :, b * T:(b + 1) * T]
                subtract(part[:, LO], t_bank[0][:, :].rearrange("p (c t) -> p c t", c=HC),
                         part[:, HI]).then_inc(xt_lo, 1)

            def ct_rest(b):
                dve.wait_ge(ct_hi, b + 1)
                part = cT[:, :, :, b * T:(b + 1) * T]
                subtract(part[:, LO], t_bank[1][:, :].rearrange("p (c t) -> p c t", c=HC),
                         part[:, HI]).then_inc(ct_lo, 1)

            for b in range(2):
                dve.wait_ge(x_in[b], 16)
                layer_stats(b, b)
            for b in range(2):
                layer_norm(b, b)
            xt_rest(0)
            ct_rest(0)
            for b in range(B):
                if b + 2 < B:
                    dve.wait_ge(x_in[b + 2], 16)
                    layer_stats(b + 2, b + 2)
                if b + 1 < B:
                    xt_rest(b + 1)
                    ct_rest(b + 1)
                if b + 2 < B:
                    dve.wait_ge(xt_ready, b + 1)
                    layer_norm(b + 2, b + 2)
                for kc in range(KC):
                    n = 2 * b + kc
                    dve.wait_ge(proj_hi, n + 1)
                    subtract(v_stage[:, b % 2, :, LO, kc, :],
                             proj_bank[n % 2][:, :].rearrange("p (g d) -> p g d", g=G),
                             v_stage[:, b % 2, :, HI, kc, :]).then_inc(proj_lo, 1)
            for u in range(G * NHALF):
                for kc in range(KC):
                    n = 2 * B + 2 * u + kc
                    dve.wait_ge(proj_hi, n + 1)
                    subtract(k_stage[:, u % 2, :, LO, kc, :],
                             proj_bank[n % 2][:, :].rearrange("p (b t) -> p b t", b=HALF),
                             k_stage[:, u % 2, :, HI, kc, :]).then_inc(proj_lo, 1)

            def q_rest(g, qd, u):
                half, h = divmod(u, QH)
                dve.wait_ge(proj_hi, count(g, UNITS, qd, PRE_UNITS + u + 1))
                cols = slice(half * 512, (half + 1) * 512)
                nc.vector.scalar_tensor_tensor(qT[:, LO, h, cols], proj_bank[u % 2][:, :], SCALE,
                                               qT[:, HI, h, cols], ALU.mult, ALU.subtract
                                               ).then_inc(proj_lo, 1)

            def row_max(g, qd, t, p):
                dve.wait_ge(s_ready[p], steps(g, qd, t + 1))
                nc.vector.tensor_reduce(nmax[:, p], s_bank[p][:, :].rearrange(
                    "p (h k) -> p h k", h=2), AX.X, ALU.max, negate=True).then_inc(max_ready[p], 1)

            def row_recip(g, qd, t, p):
                dve.wait_ge(exp_ready[p], steps(g, qd, t + 1))
                dve.wait_ge(prob_ready[p], steps(g, qd, t))
                nc.vector.reciprocal(rsum[:, p], esum[:, p]).then_inc(rsum_ready[p], 1)

            def pt_rest(g, qd, t, p):
                dve.wait_ge(pt_hi[p], steps(g, qd, t + 1))
                part = pT[:, :, :, 2 * p:2 * p + 2, :]
                subtract(part[:, LO], t_bank[p][:, :].rearrange("p (c h t) -> p c h t", c=KC, h=2),
                         part[:, HI]).then_inc(pt_lo[p], 1)

            def accumulate(g, qd, t):
                dve.wait_ge(wo_ready, steps(g, qd, t + 1))
                nc.vector.tensor_tensor(acc[:, t], wo_bank[:, :], acc[:, t], ALU.add
                                        ).then_inc(acc_ready, 1)

            def group(g, last):
                for qd in range(QUADS):
                    for u in range(QH):
                        q_rest(g, qd, u)
                        if u == 0 and qd > 0:
                            accumulate(g, qd - 1, B - 1)
                    row_max(g, qd, 0, 0)
                    row_max(g, qd, 0, 1)
                    row_recip(g, qd, 0, 0)
                    row_recip(g, qd, 0, 1)
                    for u in range(QH, UNITS):
                        q_rest(g, qd, u)
                    for t in range(B):
                        for p in range(2):
                            if t + 1 < B:
                                row_max(g, qd, t + 1, p)
                            pt_rest(g, qd, t, p)
                            if p == 1 and t >= 1:
                                accumulate(g, qd, t - 1)
                            if t + 1 < B:
                                row_recip(g, qd, t + 1, p)
                        dve.wait_ge(o_hi, steps(g, qd, t + 1))
                        subtract(oT[:, LO].rearrange("p h t -> p (h t)"), av_bank[:, :],
                                 oT[:, HI].rearrange("p h t -> p (h t)")).then_inc(o_lo, 1)
                        if last and qd == QUADS - 1 and t >= B - HC:
                            c = t - (B - HC)
                            if c == 0:
                                dve.wait_ge(ffn_in, 16)
                            else:
                                dve.wait_ge(sgn_ready, c)
                            nc.vector.tensor_scalar(neg[:, :], raw_a[:, c], 0.0, None, ALU.is_lt
                                                    ).then_inc(sgn_step, 1)
                            dve.wait_ge(sgn_step, c + 1)
                            nc.vector.scalar_tensor_tensor(raw_a[:, c], raw_a[:, c], 0.0, neg[:, :],
                                                           ALU.is_gt, ALU.subtract
                                                           ).then_inc(sgn_ready, 1)
                accumulate(g, QUADS - 1, B - 1)

            with dve.Fori(0, G - 1) as g:
                group(g, False)
            group(G - 1, True)

            def ffn_stats(b):
                dve.wait_ge(acc_ready, steps(G - 1, QUADS - 1, b + 1))
                layer_stats(B + b, b)

            def ffn_norm(b):
                if b >= 2:
                    dve.wait_ge(yt_ready, b - 1)
                layer_norm(B + b, b)

            ffn_stats(0)
            ffn_stats(1)
            ffn_norm(0)
            for i in range(B + 2):
                if i + 1 < B:
                    ffn_norm(i + 1)
                if i + 2 < B:
                    ffn_stats(i + 2)
                if 0 <= i - 1 < B:
                    b = i - 1
                    dve.wait_ge(iscale_ready, b + 1)
                    dve.wait_ge(z_hi, b)
                    nc.vector.tensor_tensor(z[:, :, :].rearrange("p c t -> p (c t)"), av_bank[:, :],
                                            yT[:, b % 2].rearrange("p c t -> p (c t)"), ALU.mult
                                            ).then_inc(z_ready, 1)
                    dve.wait_ge(z_hi, b + 1)
                    subtract(z_pair[:, b % 2, LO], z[:, :, :], z_pair[:, b % 2, HI]
                             ).then_inc(z_lo, 1)
                if i < B:
                    dve.wait_ge(logit_ready, i + 1)
                    nc.vector.tensor_reduce(gmax[:, :], s_bank[0][:, 0:E], AX.X, ALU.max,
                                            negate=True).then_inc(gmax_ready, 1)
                    dve.wait_ge(gexp_ready, i + 1)
                    nc.vector.reciprocal(grec[:, :], gsum[:, :]).then_inc(grec_ready, 1)
                    dve.wait_ge(grec_ready, i + 1)
                    dve.wait_ge(routet_ready, i)
                    nc.vector.tensor_scalar(route[:, :], gexp[:, :], grec[:, :], None, ALU.mult
                                            ).then_inc(route_ready, 1)
                if i - 2 >= 0:
                    b = i - 2
                    dve.wait_ge(ffn_ready, b + 1)
                    nc.vector.tensor_tensor(oscale[:, b % 2], ffn_bank[b % 2][:, :],
                                            oscale[:, b % 2], ALU.mult).then_inc(scaled_ready, 1)



        @block.tensor
        def _(pe):
            open_loop(pe, *s_ready, *pt_ready, av_ready, wo_ready)

            def product(dst, left, right, chunks):
                n = 0
                for a, b in TERMS:
                    for c in range(chunks):
                        last = nc.tensor.matmul(dst, left(a, c), right(b, c), start=(n == 0),
                                                stop=(n == 3 * chunks - 1))
                        n += 1
                return last

            def xt_transpose(b):
                pe.wait_ge(y_ready, b + 1)
                pe.wait_ge(xt_lo, b)
                for c in range(HC):
                    last = nc.tensor.transpose(t_bank[0][:, c * T:(c + 1) * T],
                                               y[:, b % 2, c * P:(c + 1) * P], ident[:, :])
                last.then_inc(xt_ready, 1)

            def ct_transpose(b):
                pe.wait_ge(c_in[b], 16)
                pe.wait_ge(ct_lo, b)
                for c in range(HC):
                    last = nc.tensor.transpose(t_bank[1][:, c * T:(c + 1) * T],
                                               craw[:, b, c * P:(c + 1) * P], ident[:, :])
                last.then_inc(ct_ready, 1)

            pe.wait_ge(const_ready, 2)
            xt_transpose(0)
            ct_transpose(0)
            for b in range(B):
                if b + 1 < B:
                    xt_transpose(b + 1)
                    ct_transpose(b + 1)
                if b == 0:
                    pe.wait_ge(wv_lo, HC)
                for kc, (src, lo_sem) in enumerate(((cT, ct_lo), (xT, xt_lo))):
                    n = 2 * b + kc
                    pe.wait_ge(lo_sem, b + 1)
                    if n >= 2:
                        pe.wait_ge(proj_lo, n - 1)
                    product(proj_bank[n % 2][:, :],
                            lambda s, c: src[:, s, c, b * T:(b + 1) * T],
                            lambda s, c: wv_pair[:, s, c, :], HC).then_inc(proj_ready, 1)
            pe.wait_ge(wk_lo, HC)
            for u in range(G * NHALF):
                g, half = divmod(u, NHALF)
                for kc, src in enumerate((cT, xT)):
                    n = 2 * B + 2 * u + kc
                    pe.wait_ge(proj_lo, n - 1)
                    product(proj_bank[n % 2][:, :],
                            lambda s, c: wk_pair[:, s, c, g * P:(g + 1) * P],
                            lambda s, c: src[:, s, c, half * 512:(half + 1) * 512], HC
                            ).then_inc(proj_ready, 1)

            def q_unit(g, qd, u):
                half, h = divmod(u, QH)
                if u == 0:
                    pe.wait_ge(wq_lo, count(g, HC, qd, HC))
                pe.wait_ge(proj_lo, count(g, UNITS, qd, PRE_UNITS + u - 1))
                product(proj_bank[u % 2][:, :],
                        lambda s, c: wq_pair[:, s, c, h * P:(h + 1) * P],
                        lambda s, c: xT[:, s, c, half * 512:(half + 1) * 512], HC
                        ).then_inc(proj_ready, 1)

            def scores(g, qd, t, p):
                if t % HALF == 0:
                    pe.wait_ge(proj_lo, count(g, UNITS, qd, PRE_UNITS + QH * (t // HALF) + 2 * p + 2))
                if qd == 0 and p == 0:
                    pe.wait_ge(k_in[t], 16 * (g + 1))
                pe.wait_ge(exp_ready[p], steps(g, qd, t))
                for j in range(2):
                    h = 2 * p + j
                    last = product(s_bank[p][:, j * KEYS:(j + 1) * KEYS],
                                   lambda s, c: qT[:, s, h, t * T:(t + 1) * T],
                                   lambda s, c: kg[:, t, s, :], 1)
                last.then_inc(s_ready[p], 1)

            def transposes(g, qd, t, p):
                pe.wait_ge(prob_ready[p], steps(g, qd, t + 1))
                pe.wait_ge(pt_lo[p], steps(g, qd, t))
                for kc in range(KC):
                    for j in range(2):
                        at = (2 * kc + j) * T
                        last = nc.tensor.transpose(t_bank[p][:, at:at + T],
                                                   prob[:, p, j, kc * P:(kc + 1) * P], ident[:, :])
                last.then_inc(pt_ready[p], 1)

            def attend(g, qd, t):
                if qd == 0:
                    pe.wait_ge(v_in[t], 16 * (g + 1))
                pe.wait_ge(o_lo, steps(g, qd, t))
                n = 0
                pe.wait_ge(pt_hi[1], steps(g, qd, t + 1))
                pe.wait_ge(pt_hi[0], steps(g, qd, t + 1))
                for vs, ps in ((HI, HI), (LO, HI), (HI, LO)):
                    if ps == LO:
                        pe.wait_ge(pt_lo[0], steps(g, qd, t + 1))
                        pe.wait_ge(pt_lo[1], steps(g, qd, t + 1))
                    for kc in range(KC):
                        last = nc.tensor.matmul(av_bank[:, :], vg[:, t, vs, kc, :],
                                                pT[:, ps, kc].rearrange("p h t -> p (h t)"),
                                                start=(n == 0), stop=(n == 3 * KC - 1))
                        n += 1
                last.then_inc(av_ready, 1)

            def project_out(g, qd, t, heads):
                if heads[0] == 0:
                    if t == 0:
                        pe.wait_ge(wo_lo, count(g, QH, qd, QH))
                    pe.wait_ge(acc_ready, steps(g, qd, t))
                    pe.wait_ge(o_hi, steps(g, qd, t + 1))
                for s, w in TERMS:
                    if s == LO and heads[0] == 0:
                        pe.wait_ge(o_lo, steps(g, qd, t + 1))
                    for h in heads:
                        last = nc.tensor.matmul(
                            wo_bank[:, :], oT[:, s, h, :], wo_pair[:, w, h, :],
                            start=((s, w) == TERMS[0] and h == 0),
                            stop=((s, w) == TERMS[-1] and h == QH - 1))
                if heads[-1] == QH - 1:
                    last.then_inc(wo_ready, 1)

            def group(g, last):
                for qd in range(QUADS):
                    for u in range(QH):
                        q_unit(g, qd, u)
                        if u == 0 and qd > 0:
                            project_out(g, qd - 1, B - 1, range(QH))
                    scores(g, qd, 0, 0)
                    scores(g, qd, 0, 1)
                    for u in range(QH, UNITS):
                        q_unit(g, qd, u)
                    for t in range(B):
                        for p in range(2):
                            if t + 1 < B:
                                scores(g, qd, t + 1, p)
                            transposes(g, qd, t, p)
                            if t >= 1:
                                project_out(g, qd, t - 1, range(2 * p, 2 * p + 2))
                        attend(g, qd, t)
                project_out(g, QUADS - 1, B - 1, range(QH))

            with pe.Fori(0, G - 1) as g:
                group(g, False)
            group(G - 1, True)

            pe.wait_ge(small_in, 64)
            for c in range(HC):
                last = nc.tensor.matmul(bank[0][:, c * E:(c + 1) * E], gate_sb[:, c * P:(c + 1) * P],
                                        ident[0:E, 0:E], start=True, stop=True)
            last.then_inc(gatet_ready, 1)
            pe.wait_ge(sgn_ready, HC)
            for c in range(HC):
                if c >= 2:
                    pe.wait_ge(sgnt_copied, c - 1)
                for r in range(HC):
                    last = nc.tensor.transpose(proj_bank[c % 2][:, r * P:(r + 1) * P],
                                               raw_a[:, r, c * P:(c + 1) * P], ident[:, :])
                last.then_inc(sgnt_ready, 1)
            pe.wait_ge(gatet_copied, 1)
            pe.wait_ge(sgnt_copied, HC)
            pe.wait_ge(acc_ready, steps(G - 1, QUADS - 1, B))
            for i in range(B + 2):
                if i < B:
                    pe.wait_ge(y_ready, B + i + 1)
                    if i >= 2:
                        pe.wait_ge(yt_copied, i - 1)
                    for c in range(HC):
                        last = nc.tensor.transpose(t_bank[i % 2][:, c * T:(c + 1) * T],
                                                   y[:, i % 2, c * P:(c + 1) * P], ident[:, :])
                    last.then_inc(yt_ready, 1)
                if 0 <= i - 1 < B:
                    b = i - 1
                    pe.wait_ge(route_ready, b + 1)
                    pe.wait_ge(routet_copied, b)
                    nc.tensor.matmul(proj_bank[0][0:E, 0:T], route[:, :], ident[:, :], start=True,
                                     stop=True).then_inc(routet_ready, 1)
                if i < B:
                    pe.wait_ge(yt_copied, i + 1)
                    pe.wait_ge(gexp_ready, i)
                    for c in range(HC):
                        last = nc.tensor.matmul(s_bank[0][:, 0:E], yT[:, i % 2, c, :],
                                                gateT[:, c, :], start=(c == 0), stop=(c == HC - 1))
                    last.then_inc(logit_ready, 1)
                if 0 <= i - 1 < B:
                    b = i - 1
                    pe.wait_ge(routet_copied, b + 1)
                    pe.wait_ge(z_ready, b)
                    for c in range(HC):
                        last = nc.tensor.matmul(av_bank[:, c * T:(c + 1) * T],
                                                ics[:, c * P:(c + 1) * P], routeT[:, :],
                                                start=True, stop=True)
                    last.then_inc(iscale_ready, 1)
                    pe.wait_ge(oscale_copied, b)
                    nc.tensor.matmul(wo_bank[:, :], routeT[:, :], ocs[:, :], start=True, stop=True
                                     ).then_inc(oscale_ready, 1)
                if i - 2 >= 0:
                    b = i - 2
                    pe.wait_ge(z_hi, b + 1)
                    if b >= 2:
                        pe.wait_ge(scaled_ready, b - 1)
                    for s in (HI, LO):
                        if s == LO:
                            pe.wait_ge(z_lo, b + 1)
                        for c in range(HC):
                            last = nc.tensor.matmul(ffn_bank[b % 2][:, :], z_pair[:, b % 2, s, c, :],
                                                    sgnT[:, c, :], start=(s == HI and c == 0),
                                                    stop=(s == LO and c == HC - 1))
                    last.then_inc(ffn_ready, 1)


_INS = ["x", "ctx_4096", "L0_xattn_Wq", "L0_xattn_Wk", "L0_xattn_Wv", "L0_xattn_Wo", "L0_ffn_weight",
        "L0_ffn_bias", "L0_ffn_gate_w", "L0_ffn_in_channel_scale", "L0_ffn_out_channel_scale"]


def kernel(**inputs):
    import numpy as np
    import concourse.bacc as bacc
    from concourse.bass_utils import run_bass_kernel_spmd

    nc = bacc.Bacc("TRN2", target_bir_lowering=False, num_devices=1)
    arrays, args = {}, []
    for name in _INS:
        a = np.ascontiguousarray(inputs[name])
        arrays[f"in_{name}"] = a
        args.append(nc.dram_tensor(f"in_{name}", a.shape, mybir.dt.from_np(a.dtype),
                                   kind="ExternalInput").ap())
    args.append(nc.dram_tensor("out_y", arrays["in_x"].shape, mybir.dt.float32,
                               kind="ExternalOutput").ap())
    xattn_ffn(nc, *args)
    result = run_bass_kernel_spmd(nc, [arrays], core_ids=[0])
    return result.results[0]["out_y"]
```

```python
import concourse.bass as bass
from concourse import mybir
from contextlib import ExitStack

HI, LO = 0, 1
TERMS = ((HI, HI), (HI, LO), (LO, HI))


def xattn_ffn(nc, x, ctx, wq, wk, wv, wo, ffn_w, ffn_b, gate_w, in_cs, out_cs, out):
    fp32 = mybir.dt.float32
    f32r = mybir.dt.float32r
    ALU = mybir.AluOpType
    ACT = mybir.ActivationFunctionType
    AX = mybir.AxisListType

    P = 128
    B, T, D = x.shape
    HC = D // P
    HEADS = wq.shape[1] // P
    G = wk.shape[1] // P
    QH = 4
    QUADS = HEADS // G // QH
    KEYS = 2 * T
    KC = KEYS // P
    E = gate_w.shape[0]
    HALF = 4
    NHALF = B // HALF
    UNITS = NHALF * QH
    PRE_UNITS = 2 * B + 2 * G * NHALF
    SCALE = float(P) ** -0.5
    EPS = 1e-5
    OS = 4

    es = ExitStack()
    with es:
        def sb(stack, name, shape, dt=fp32):
            return stack.enter_context(nc.sbuf_tensor(name, shape, dt))

        def sem(name):
            return es.enter_context(nc.semaphore(name))

        k_park = nc.dram_tensor("k_park", (G, P, B, 2, KEYS), fp32).ap()
        v_park = nc.dram_tensor("v_park", (G, P, B, 2, KC, P), fp32).ap()

        xT = sb(es, "xT", [P, 2, HC, B * T], f32r)
        acc = sb(es, "acc", [P, B, D])
        wq_pair = sb(es, "wq_pair", [P, 2, HC, QH * P], f32r)
        raw_a = sb(es, "raw_a", [P, HC, D])
        raw_b = sb(es, "raw_b", [P, QH, D])
        ident = sb(es, "ident", [P, P])
        y = sb(es, "y", [P, 2, D])
        stats = sb(es, "stats", [P, 2, 6])
        mv = sb(es, "mv", [P, 2 * B, 2])
        vare = sb(es, "vare", [P, 2 * B])
        rstd0 = sb(es, "rstd0", [P, 2 * B])
        nwt = sb(es, "nwt", [P, 2 * B])
        nwt2 = sb(es, "nwt2", [P, 2 * B])
        nwt3 = sb(es, "nwt3", [P, 2 * B])
        rstd = sb(es, "rstd", [P, 2 * B])
        neg_half = sb(es, "neg_half", [P, 1])
        small = sb(es, "small", [P, D])
        scales = sb(es, "scales", [P, 2, D], f32r)
        nmax = sb(es, "nmax", [P, 2, 2])
        esum = sb(es, "esum", [P, 2, 2])
        rsum = sb(es, "rsum", [P, 2, 2])
        bias_b = sb(es, "bias_b", [P, D])
        gateT = sb(es, "gateT", [P, HC, E])
        with ExitStack() as pre:
            cT = sb(pre, "cT", [P, 2, HC, B * T], f32r)
            wv_pair = sb(pre, "wv_pair", [P, 2, HC, D], f32r)
            craw = sb(pre, "craw", [P, B, D])
            wk_pair = sb(pre, "wk_pair", [P, 2, HC, D], f32r)
            v_stage = sb(pre, "v_stage", [P, 2, G, 2, KC, P], f32r)
            k_stage = sb(pre, "k_stage", [P, 2, HALF, 2, KC, P], f32r)
        with ExitStack() as att:
            qT = sb(att, "qT", [P, 2, QH, B * T], f32r)
            wo_pair = sb(att, "wo_pair", [P, 2, QH, D], f32r)
            kg = sb(att, "kg", [P, B, 2, KEYS], f32r)
            vg = sb(att, "vg", [P, B, 2, KC, P], f32r)
            prob = sb(att, "prob", [P, 2, 2, KEYS])
            pT = sb(att, "pT", [P, 2, KC, QH, T], f32r)
            oT = sb(att, "oT", [P, 2, QH, T], f32r)
            yT = sb(att, "yT", [P, 2, HC, T])
            oscale = sb(att, "oscale", [P, OS, D])
            gmax = sb(att, "gmax", [P, 1])
            gexp = sb(att, "gexp", [P, E])
            gsum = sb(att, "gsum", [P, 1])
            grec = sb(att, "grec", [P, 1])
            route = sb(att, "route", [P, E])
            route3 = sb(att, "route3", [P, P])
            routeT = sb(att, "routeT", [P, T], f32r)
        sgnT = wq_pair[:, HI]
        z_pair = wq_pair[:, LO].rearrange("p (n s) (c t) -> p n s c t", n=2, c=HC)

        bank = [es.enter_context(nc.psum_tensor(f"bank{i}", [P, 512], fp32)) for i in range(8)]
        s_bank, t_bank, proj_bank = bank[0:2], bank[2:4], bank[6:8]
        av_bank, wo_bank = bank[4], bank[5]
        scale_bank = [proj_bank[0]] * (B - 2) + t_bank
        route_bank = [proj_bank[1]] * (B - 2) + s_bank
        prod_bank = [proj_bank[1]] * (B - 4) + [av_bank, wo_bank, proj_bank[1], proj_bank[0]]

        x_in = [sem(f"x_in{b}") for b in range(B)]
        c_in = [sem(f"c_in{b}") for b in range(B)]
        wv_in = [sem(f"wv_in{c}") for c in range(HC)]
        wk_in, wq_in, wo_in, gate_in, bias_in, scales_in, ffn_in = (
            sem(n) for n in ("wk_in", "wq_in", "wo_in", "gate_in", "bias_in", "scales_in", "ffn_in"))
        k_in = [sem(f"k_in{b}") for b in range(B)]
        v_in = [sem(f"v_in{b}") for b in range(B)]
        v_parked = [sem(f"v_parked{i}") for i in range(2)]
        k_parked = [sem(f"k_parked{i}") for i in range(2)]
        out_stored = sem("out_stored")
        zeroed, const_ready = sem("zeroed"), sem("const_ready")
        scales_hi, scales_ready, route3_zeroed = (
            sem("scales_hi"), sem("scales_ready"), sem("route3_zeroed"))
        wv_hi, wv_lo, wk_hi, wk_lo, wq_hi, wq_lo, wo_hi, wo_lo = (
            sem(n) for n in ("wv_hi", "wv_lo", "wk_hi", "wk_lo", "wq_hi", "wq_lo", "wo_hi", "wo_lo"))
        stats_ready, mv_ready, rstd_ready, rstd_step, y_ready = (
            sem(n) for n in ("stats_ready", "mv_ready", "rstd_ready", "rstd_step", "y_ready"))
        xt_ready, xt_hi, xt_lo, ct_ready, ct_hi, ct_lo = (
            sem(n) for n in ("xt_ready", "xt_hi", "xt_lo", "ct_ready", "ct_hi", "ct_lo"))
        proj_ready, proj_hi, proj_lo = sem("proj_ready"), sem("proj_hi"), sem("proj_lo")
        s_ready, max_ready, exp_ready, rsum_ready, prob_ready, pt_ready, pt_hi, pt_lo = (
            [sem(f"{n}{p}") for p in range(2)]
            for n in ("s_ready", "max_ready", "exp_ready", "rsum_ready", "prob_ready", "pt_ready",
                      "pt_hi", "pt_lo"))
        av_ready, o_hi, o_lo, wo_ready, acc_ready = (
            sem(n) for n in ("av_ready", "o_hi", "o_lo", "wo_ready", "acc_ready"))
        sgn_step, sgn_ready, sgnt_ready, sgnt_copied, gatet_ready, gatet_copied = (
            sem(n) for n in ("sgn_step", "sgn_ready", "sgnt_ready", "sgnt_copied", "gatet_ready",
                             "gatet_copied"))
        yt_ready, yt_copied, logit_ready, gmax_ready, gexp_ready, grec_ready, route_ready = (
            sem(n) for n in ("yt_ready", "yt_copied", "logit_ready", "gmax_ready", "gexp_ready",
                             "grec_ready", "route_ready"))
        routet_ready, routet_copied, iscale_ready, oscale_ready, oscale_copied = (
            sem(n) for n in ("routet_ready", "routet_copied", "iscale_ready", "oscale_ready",
                             "oscale_copied"))
        route_split = sem("route_split")
        z_ready, z_hi, z_lo, ffn_ready, scaled_ready, bias_added, out_ready, last_out_ready = (
            sem(n) for n in ("z_ready", "z_hi", "z_lo", "ffn_ready", "scaled_ready", "bias_added",
                             "out_ready", "last_out_ready"))

        block = es.enter_context(nc.Block())

        def count(g, per_quad, qd, k):
            return g * (QUADS * per_quad) + (per_quad * qd + k)

        def steps(g, qd, k):
            return g * (QUADS * B) + (B * qd + k + 1)

        def open_loop(engine, *semaphores):
            for s in semaphores:
                engine.sem_inc(s, 1)

        @block.sync
        def _(sp):
            wq_v = wq.rearrange("(c p) n -> p c n", p=P)
            wo_v = wo.rearrange("(h p) n -> p h n", p=P)

            def words(pair):
                return pair.bitcast(fp32)

            def load_x(b):
                sp.dma_start(acc[:, b, :], x[b]).then_inc(x_in[b], 16)

            def load_c(b):
                sp.dma_start(craw[:, b, :], ctx[b]).then_inc(c_in[b], 16)

            def load_wq(g, quad):
                cols = bass.ds(g * (QUADS * QH * P) + quad * QH * P, QH * P)
                sp.dma_start(raw_a[:, :, :], wq_v[:, :, cols]).then_inc(wq_in, 16)

            def load_wo(g, quad):
                heads = bass.ds(g * (QUADS * QH) + quad * QH, QH)
                sp.dma_start(raw_b[:, :, :], wo_v[:, heads, :]).then_inc(wo_in, 16)

            def load_kv(g, b):
                sp.dma_start(words(kg[:, b, :, :]), k_park[bass.ds(g, 1), :, b, :, :].rearrange(
                    "a p s k -> p (a s) k")).then_inc(k_in[b], 16)
                sp.dma_start(words(vg[:, b, :, :, :]), v_park[bass.ds(g, 1), :, b, :, :, :].rearrange(
                    "a p s c k -> p (a s) c k")).then_inc(v_in[b], 16)

            load_x(0)
            load_c(0)
            for c in range(HC):
                sp.dma_start(raw_a[:, c, :], wv[c * P:(c + 1) * P, :]).then_inc(wv_in[c], 16)
            for b in range(1, B):
                load_c(b)
                load_x(b)
                if b == 4:
                    sp.dma_start(raw_b[:, :, :], wk.rearrange("(c p) n -> p c n", p=P)
                                 ).then_inc(wk_in, 16)
            sp.dma_start(small[0:E, :], gate_w).then_inc(gate_in, 16)
            sp.dma_start(bias_b[:, :], ffn_b.rearrange("(a n) -> a n", a=1).broadcast_to((P, D))
                         ).then_inc(bias_in, 16)
            sp.wait_ge(wv_lo, HC)
            load_wq(0, 0)
            for b in range(B):
                sp.wait_ge(proj_lo, 2 * b + 2)
                sp.dma_start(v_park[:, :, b].rearrange("g p s c k -> p g (s c k)"),
                             words(v_stage[:, b % 2]).rearrange("p g s c k -> p g (s c k)")
                             ).then_inc(v_parked[b % 2], 16)
            sp.wait_ge(wk_lo, HC)
            load_wo(0, 0)
            sp.wait_ge(xt_ready, B)
            for part, src in enumerate((in_cs, out_cs)):
                for r in range(3):
                    sp.dma_start(y[32 * r:32 * r + E, part, :], src).then_inc(scales_in, 16)
            for u in range(G * NHALF):
                g, half = divmod(u, NHALF)
                sp.wait_ge(proj_lo, 2 * B + 2 * u + 2)
                sp.dma_start(k_park[g, :, half * HALF:(half + 1) * HALF].rearrange(
                    "p b s k -> p (b s k)"), words(k_stage[:, u % 2]).rearrange("p b s c k -> p (b s c k)")
                    ).then_inc(k_parked[u % 2], 16)
            for i in range(2):
                sp.wait_ge(v_parked[i], 16 * (B // 2))
                sp.wait_ge(k_parked[i], 16 * (G * NHALF // 2))
            sp.wait_ge(proj_ready, PRE_UNITS)
            for b in range(B):
                load_kv(0, b)

            def group(g, last):
                for qd in range(QUADS):
                    if last and qd == QUADS - 1:
                        sp.wait_ge(wq_lo, count(g, HC, qd, HC))
                        sp.dma_start(raw_a[:, :, :], ffn_w.rearrange("(c p) n -> p c n", p=P)
                                     ).then_inc(ffn_in, 16)
                        break
                    sp.wait_ge(wq_lo, count(g, HC, qd, HC))
                    load_wq(g, qd + 1)
                    sp.wait_ge(wo_lo, count(g, QH, qd, QH))
                    load_wo(g, qd + 1)
                if not last:
                    qd = QUADS - 1
                    for b in range(B):
                        for p in range(2):
                            sp.wait_ge(s_ready[p], steps(g, qd, b + 1))
                        sp.wait_ge(av_ready, steps(g, qd, b + 1))
                        load_kv(g + 1, b)

            with sp.Fori(0, G - 1) as g:
                group(g, False)
            group(G - 1, True)

            for b in range(B):
                if b < B - 1:
                    sp.wait_ge(out_ready, b + 1)
                else:
                    sp.wait_ge(last_out_ready, 1)
                sp.dma_start(out[b], acc[:, b, :]).then_inc(out_stored, 16)
            sp.wait_ge(out_stored, 16 * B)

        @block.gpsimd
        def _(pool):
            open_loop(pool, *prob_ready)
            pool.memset(ident[:, :], 0.0).then_inc(zeroed, 1)
            pool.memset(neg_half[:, :], -0.5).then_inc(const_ready, 1)
            pool.memset(scales[:, :, :].bitcast(fp32), 0.0).then_inc(zeroed, 1)
            pool.wait_ge(zeroed, 1)
            pool.affine_select(out=ident[:, :], in_=ident[:, :], compare_op=ALU.not_equal, fill=1.0,
                               base=0, pattern=[[-1, P]], channel_multiplier=1
                               ).then_inc(const_ready, 1)

            def split_lo(pair, raw, c, hi_sem, hi_count, lo_sem):
                pool.wait_ge(hi_sem, hi_count)
                nc.gpsimd.tensor_tensor(pair[:, LO, c, :], raw[:, c, :], pair[:, HI, c, :],
                                        ALU.subtract).then_inc(lo_sem, 1)

            def make_rstd(i):
                step = 4 * i
                col = slice(i, i + 1)
                pool.wait_ge(mv_ready, i + 1)
                nc.gpsimd.tensor_scalar(vare[:, col], mv[:, i, 1:2], EPS, None, ALU.add
                                        ).then_inc(rstd_step, 1)
                pool.wait_ge(rstd_step, step + 1)
                nc.gpsimd.tensor_tensor(rstd0[:, col], vare[:, col], neg_half[:, :], ALU.pow
                                        ).then_inc(rstd_step, 1)
                pool.wait_ge(rstd_step, step + 2)
                nc.gpsimd.tensor_tensor(nwt[:, col], rstd0[:, col], rstd0[:, col], ALU.mult
                                        ).then_inc(rstd_step, 1)
                pool.wait_ge(rstd_step, step + 3)
                nc.gpsimd.tensor_tensor(nwt2[:, col], nwt[:, col], vare[:, col], ALU.mult
                                        ).then_inc(rstd_step, 1)
                pool.wait_ge(rstd_step, step + 4)
                nc.gpsimd.tensor_scalar(nwt3[:, col], nwt2[:, col], -0.5, 1.5, ALU.mult, ALU.add
                                        ).then_inc(rstd_ready, 1)
                pool.wait_ge(rstd_ready, 2 * i + 1)
                nc.gpsimd.tensor_tensor(rstd[:, col], rstd0[:, col], nwt3[:, col], ALU.mult
                                        ).then_inc(rstd_ready, 1)

            pool.wait_ge(const_ready, 2)
            for b in range(B):
                make_rstd(b)
            for c in range(HC):
                split_lo(wk_pair, raw_b, c, wk_hi, c + 1, wk_lo)
            for c in range(HC):
                split_lo(wq_pair, raw_a, c, wq_hi, c + 1, wq_lo)

            def normalise(g, qd, t, p):
                pool.wait_ge(exp_ready[p], steps(g, qd, t + 1))
                pool.wait_ge(rsum_ready[p], steps(g, qd, t + 1))
                nc.gpsimd.tensor_tensor(prob[:, p], prob[:, p],
                                        rsum[:, p].unsqueeze(2).to_broadcast([P, 2, KEYS]),
                                        ALU.mult).then_inc(prob_ready[p], 1)

            def bias_add(b):
                pool.wait_ge(y_ready, B + b + 1)
                nc.gpsimd.tensor_tensor(acc[:, b], acc[:, b], bias_b[:, :], ALU.add
                                        ).then_inc(bias_added, 1)

            def ffn_add(b):
                pool.wait_ge(scaled_ready, b + 1)
                pool.wait_ge(bias_added, b + 1)
                nc.gpsimd.tensor_tensor(acc[:, b], acc[:, b], oscale[:, b % OS], ALU.add
                                        ).then_inc(out_ready, 1)

            def ffn_step(t):
                if t >= 1:
                    make_rstd(B + t - 1)
                if t >= 2:
                    bias_add(t - 2)
                if t >= 5:
                    ffn_add(t - 5)

            def group(g, last):
                for qd in range(QUADS):
                    final = last and qd == QUADS - 1
                    for h in range(QH):
                        split_lo(wo_pair, raw_b, h, wo_hi, count(g, QH, qd, h + 1), wo_lo)
                    for p in range(2):
                        normalise(g, qd, 0, p)
                    for t in range(B):
                        if t + 1 < B:
                            for p in range(2):
                                normalise(g, qd, t + 1, p)
                        if 1 <= t <= HC and not final:
                            split_lo(wq_pair, raw_a, t - 1, wq_hi, count(g, HC, qd, HC + t), wq_lo)
                        if final:
                            ffn_step(t)

            with pool.Fori(0, G - 1) as g:
                group(g, False)
            pool.memset(route3[:, :], 0.0).then_inc(route3_zeroed, 1)
            pool.wait_ge(bias_in, 16)
            group(G - 1, True)
            make_rstd(2 * B - 1)
            ffn_add(B - 5)
            bias_add(B - 2)
            bias_add(B - 1)
            for b in range(B - 4, B - 1):
                ffn_add(b)

        @block.scalar
        def _(act):
            open_loop(act, *exp_ready, *pt_hi, o_hi)

            def copy(dst, src):
                return nc.scalar.activation(dst, src, ACT.Copy)

            def split_hi(pair, raw, c, sem_):
                copy(pair[:, HI, c, :], raw[:, c, :]).then_inc(sem_, 1)

            def xt_half(b):
                act.wait_ge(xt_ready, b + 1)
                copy(xT[:, HI, :, b * T:(b + 1) * T],
                     t_bank[0][:, :].rearrange("p (c t) -> p c t", c=HC)).then_inc(xt_hi, 1)

            def ct_half(b):
                act.wait_ge(ct_ready, b + 1)
                copy(cT[:, HI, :, b * T:(b + 1) * T],
                     t_bank[1][:, :].rearrange("p (c t) -> p c t", c=HC)).then_inc(ct_hi, 1)

            ct_half(0)
            for c in range(HC):
                act.wait_ge(wv_in[c], 16)
                split_hi(wv_pair, raw_a, c, wv_hi)
            xt_half(0)
            for b in range(B):
                if b >= 2:
                    act.wait_ge(v_parked[b % 2], 16 * (b // 2))
                for kc in range(KC):
                    n = 2 * b + kc
                    if b + 1 < B:
                        (ct_half, xt_half)[kc](b + 1)
                    act.wait_ge(proj_ready, n + 1)
                    copy(v_stage[:, b % 2, :, HI, kc, :],
                         proj_bank[n % 2][:, :].rearrange("p (g d) -> p g d", g=G)
                         ).then_inc(proj_hi, 1)
                if b == 5:
                    act.wait_ge(wk_in, 16)
                    for c in range(HC):
                        split_hi(wk_pair, raw_b, c, wk_hi)
            act.wait_ge(gatet_ready, 1)
            copy(gateT[:, :, :], t_bank[0][:, 0:HC * E].rearrange("p (c e) -> p c e", c=HC)
                 ).then_inc(gatet_copied, 1)
            act.wait_ge(wq_in, 16)
            for c in range(HC):
                split_hi(wq_pair, raw_a, c, wq_hi)
            for u in range(G * NHALF):
                if u >= 2:
                    act.wait_ge(k_parked[u % 2], 16 * (u // 2))
                for kc in range(KC):
                    n = 2 * B + 2 * u + kc
                    act.wait_ge(proj_ready, n + 1)
                    copy(k_stage[:, u % 2, :, HI, kc, :],
                         proj_bank[n % 2][:, :].rearrange("p (b t) -> p b t", b=HALF)
                         ).then_inc(proj_hi, 1)
            act.wait_ge(scales_in, 96)
            act.wait_ge(zeroed, 2)
            for r in range(3):
                rows = slice(32 * r, 32 * r + E)
                copy(scales[rows], y[rows]).then_inc(scales_hi, 1)
            for i in range(2):
                act.wait_ge(v_parked[i], 16 * (B // 2))

            def q_half(g, qd, u):
                half, h = divmod(u, QH)
                act.wait_ge(proj_ready, count(g, UNITS, qd, PRE_UNITS + u + 1))
                act.wait_ge(s_ready[h // 2], steps(g, qd, 0))
                nc.scalar.activation(qT[:, HI, h, half * 512:(half + 1) * 512],
                                     proj_bank[u % 2][:, :], ACT.Copy, scale=SCALE
                                     ).then_inc(proj_hi, 1)

            def exps(g, qd, t, p):
                act.wait_ge(max_ready[p], steps(g, qd, t + 1))
                act.wait_ge(pt_ready[p], steps(g, qd, t))
                for j in range(2):
                    ins = nc.scalar.activation(prob[:, p, j], s_bank[p][:, j * KEYS:(j + 1) * KEYS],
                                               ACT.Exp, bias=nmax[:, p, j:j + 1],
                                               accum_out=esum[:, p, j:j + 1])
                ins.then_inc(exp_ready[p], 1)

            def pt_half(g, qd, t, p):
                act.wait_ge(pt_ready[p], steps(g, qd, t + 1))
                act.wait_ge(av_ready, steps(g, qd, t))
                copy(pT[:, HI, :, 2 * p:2 * p + 2, :],
                     t_bank[p][:, :].rearrange("p (c h t) -> p c h t", c=KC, h=2)
                     ).then_inc(pt_hi[p], 1)

            def o_half(g, qd, t):
                act.wait_ge(av_ready, steps(g, qd, t + 1))
                act.wait_ge(wo_ready, steps(g, qd, t))
                copy(oT[:, HI].rearrange("p h t -> p (h t)"), av_bank[:, :]).then_inc(o_hi, 1)

            def sgn_copy(c):
                act.wait_ge(sgnt_ready, c + 1)
                copy(sgnT[:, c, :], proj_bank[c % 2][:, :]).then_inc(sgnt_copied, 1)

            def routet_copy(b):
                act.wait_ge(routet_ready, b + 1)
                act.wait_ge(oscale_ready, b)
                copy(routeT[:, :], route_bank[b][:, 0:T]).then_inc(routet_copied, 1)

            def oscale_copy(b):
                act.wait_ge(oscale_ready, b + 1)
                if b >= OS:
                    act.wait_ge(out_ready, b - OS + 1)
                copy(oscale[:, b % OS], route_bank[b][:, :]).then_inc(oscale_copied, 1)

            def z_half(b):
                act.wait_ge(z_ready, b + 1)
                if b >= 2:
                    act.wait_ge(ffn_ready, b - 1)
                copy(z_pair[:, b % 2, HI], small[:, :].rearrange("p (c t) -> p c t", c=HC)
                     ).then_inc(z_hi, 1)

            def yt_copy(b):
                act.wait_ge(yt_ready, b + 1)
                if b >= 2:
                    act.wait_ge(z_ready, b - 1)
                    act.wait_ge(logit_ready, b - 1)
                copy(yT[:, b % 2], scale_bank[b][:, :].rearrange("p (c t) -> p c t", c=HC)
                     ).then_inc(yt_copied, 1)

            def gate_exp(b):
                act.wait_ge(gmax_ready, b + 1)
                nc.scalar.activation(gexp[:, :], route_bank[b][:, 0:E], ACT.Exp, bias=gmax[:, :],
                                     accum_out=gsum[:, :]).then_inc(gexp_ready, 1)

            def group(g, last):
                for qd in range(QUADS):
                    final = last and qd == QUADS - 1
                    nxt = (g, qd + 1) if qd + 1 < QUADS else (g + 1, 0)
                    q_half(g, qd, 2)
                    q_half(g, qd, 3)
                    act.wait_ge(wo_in, 16 * count(g, 1, qd, 1))
                    act.wait_ge(wo_ready, steps(g, qd, 0))
                    for h in range(QH):
                        split_hi(wo_pair, raw_b, h, wo_hi)
                    exps(g, qd, 0, 0)
                    q_half(g, qd, 4)
                    exps(g, qd, 0, 1)
                    q_half(g, qd, 5)
                    q_half(g, qd, 6)
                    for t in range(B):
                        if final and t >= 3:
                            gate_exp(t - 3)
                        pt_half(g, qd, t, 0)
                        if t + 1 < B:
                            exps(g, qd, t + 1, 0)
                        if final and t == 1:
                            sgn_copy(0)
                            sgn_copy(1)
                        pt_half(g, qd, t, 1)
                        if final and t >= 3:
                            routet_copy(t - 3)
                        if t + 1 < B:
                            exps(g, qd, t + 1, 1)
                        if final and t == 1:
                            sgn_copy(2)
                            sgn_copy(3)
                        if final and t >= 3:
                            oscale_copy(t - 3)
                            z_half(t - 3)
                        if t == 0:
                            q_half(g, qd, UNITS - 1)
                        if t == B - 1 and not final:
                            q_half(*nxt, 0)
                        if 1 <= t <= HC and not final:
                            if t == 1:
                                act.wait_ge(wq_in, 16 * count(g, 1, qd, 2))
                            split_hi(wq_pair, raw_a, t - 1, wq_hi)
                        o_half(g, qd, t)
                        if final and t >= 2:
                            yt_copy(t - 2)
                    if not final:
                        q_half(*nxt, 1)

            q_half(0, 0, 0)
            q_half(0, 0, 1)
            with act.Fori(0, G - 1) as g:
                group(g, False)
            group(G - 1, True)
            gate_exp(B - 3)
            yt_copy(B - 2)
            routet_copy(B - 3)
            oscale_copy(B - 3)
            gate_exp(B - 2)
            z_half(B - 3)
            routet_copy(B - 2)
            yt_copy(B - 1)
            oscale_copy(B - 2)
            z_half(B - 2)
            gate_exp(B - 1)
            routet_copy(B - 1)
            oscale_copy(B - 1)
            z_half(B - 1)

        @block.vector
        def _(dve):
            open_loop(dve, *max_ready, *rsum_ready, *pt_lo, o_lo, acc_ready)

            def subtract(dst, a, b):
                return nc.vector.tensor_tensor(dst, a, b, ALU.subtract)

            def layer_stats(i, b):
                nc.vector.bn_stats(stats[:, i % 2], acc[:, b, :]).then_inc(stats_ready, 1)
                dve.wait_ge(stats_ready, i + 1)
                nc.vector.bn_aggr(mv[:, i], stats[:, i % 2]).then_inc(mv_ready, 1)

            def layer_norm(i, b):
                dve.wait_ge(rstd_ready, 2 * i + 2)
                nc.vector.tensor_scalar(y[:, i % 2], acc[:, b, :], mv[:, i, 0:1], rstd[:, i:i + 1],
                                        ALU.subtract, ALU.mult).then_inc(y_ready, 1)

            def xt_rest(b):
                dve.wait_ge(xt_hi, b + 1)
                part = xT[:, :, :, b * T:(b + 1) * T]
                subtract(part[:, LO], t_bank[0][:, :].rearrange("p (c t) -> p c t", c=HC),
                         part[:, HI]).then_inc(xt_lo, 1)

            def ct_rest(b):
                dve.wait_ge(ct_hi, b + 1)
                part = cT[:, :, :, b * T:(b + 1) * T]
                subtract(part[:, LO], t_bank[1][:, :].rearrange("p (c t) -> p c t", c=HC),
                         part[:, HI]).then_inc(ct_lo, 1)

            dve.wait_ge(x_in[0], 16)
            layer_stats(0, 0)
            ct_rest(0)
            layer_norm(0, 0)
            for c in range(HC):
                dve.wait_ge(wv_hi, c + 1)
                subtract(wv_pair[:, LO, c, :], raw_a[:, c, :], wv_pair[:, HI, c, :]
                         ).then_inc(wv_lo, 1)
            xt_rest(0)
            dve.wait_ge(x_in[1], 16)
            layer_stats(1, 1)
            layer_norm(1, 1)
            for b in range(B):
                for kc in range(KC):
                    n = 2 * b + kc
                    if b + 1 < B:
                        (ct_rest, xt_rest)[kc](b + 1)
                    if b + 2 < B:
                        if kc == 0:
                            dve.wait_ge(x_in[b + 2], 16)
                            layer_stats(b + 2, b + 2)
                        else:
                            dve.wait_ge(xt_ready, b + 1)
                            layer_norm(b + 2, b + 2)
                    dve.wait_ge(proj_hi, n + 1)
                    subtract(v_stage[:, b % 2, :, LO, kc, :],
                             proj_bank[n % 2][:, :].rearrange("p (g d) -> p g d", g=G),
                             v_stage[:, b % 2, :, HI, kc, :]).then_inc(proj_lo, 1)
            for u in range(G * NHALF):
                for kc in range(KC):
                    n = 2 * B + 2 * u + kc
                    dve.wait_ge(proj_hi, n + 1)
                    subtract(k_stage[:, u % 2, :, LO, kc, :],
                             proj_bank[n % 2][:, :].rearrange("p (b t) -> p b t", b=HALF),
                             k_stage[:, u % 2, :, HI, kc, :]).then_inc(proj_lo, 1)

            dve.wait_ge(scales_hi, 3)
            subtract(scales[32:32 + E], y[32:32 + E], scales[32:32 + E]).then_inc(scales_ready, 1)

            def q_rest(g, qd, u):
                half, h = divmod(u, QH)
                dve.wait_ge(proj_hi, count(g, UNITS, qd, PRE_UNITS + u + 1))
                cols = slice(half * 512, (half + 1) * 512)
                nc.vector.scalar_tensor_tensor(qT[:, LO, h, cols], proj_bank[u % 2][:, :], SCALE,
                                               qT[:, HI, h, cols], ALU.mult, ALU.subtract
                                               ).then_inc(proj_lo, 1)

            def row_max(g, qd, t, p):
                dve.wait_ge(s_ready[p], steps(g, qd, t + 1))
                nc.vector.tensor_reduce(nmax[:, p], s_bank[p][:, :].rearrange(
                    "p (h k) -> p h k", h=2), AX.X, ALU.max, negate=True).then_inc(max_ready[p], 1)

            def row_recip(g, qd, t, p):
                dve.wait_ge(exp_ready[p], steps(g, qd, t + 1))
                dve.wait_ge(prob_ready[p], steps(g, qd, t))
                nc.vector.reciprocal(rsum[:, p], esum[:, p]).then_inc(rsum_ready[p], 1)

            def pt_rest(g, qd, t, p):
                dve.wait_ge(pt_hi[p], steps(g, qd, t + 1))
                part = pT[:, :, :, 2 * p:2 * p + 2, :]
                subtract(part[:, LO], t_bank[p][:, :].rearrange("p (c h t) -> p c h t", c=KC, h=2),
                         part[:, HI]).then_inc(pt_lo[p], 1)

            def accumulate(g, qd, t):
                dve.wait_ge(wo_ready, steps(g, qd, t + 1))
                nc.vector.tensor_tensor(acc[:, t], wo_bank[:, :], acc[:, t], ALU.add
                                        ).then_inc(acc_ready, 1)

            def o_rest(g, qd, t):
                dve.wait_ge(o_hi, steps(g, qd, t + 1))
                subtract(oT[:, LO].rearrange("p h t -> p (h t)"), av_bank[:, :],
                         oT[:, HI].rearrange("p h t -> p (h t)")).then_inc(o_lo, 1)

            def sgn(c):
                if c == 0:
                    dve.wait_ge(ffn_in, 16)
                    dve.wait_ge(scales_ready, 1)
                else:
                    dve.wait_ge(sgn_ready, c)
                nc.vector.tensor_scalar(y[:, 0], raw_a[:, c], 0.0, None, ALU.is_lt
                                        ).then_inc(sgn_step, 1)
                dve.wait_ge(sgn_step, c + 1)
                nc.vector.scalar_tensor_tensor(raw_a[:, c], raw_a[:, c], 0.0, y[:, 0],
                                               ALU.is_gt, ALU.subtract).then_inc(sgn_ready, 1)

            def ffn_stats(b):
                dve.wait_ge(acc_ready, steps(G - 1, QUADS - 1, b + 1))
                layer_stats(B + b, b)

            def ffn_norm(b):
                if b >= 2:
                    dve.wait_ge(yt_ready, b - 1)
                layer_norm(B + b, b)

            def z_make(b):
                dve.wait_ge(iscale_ready, b + 1)
                if b >= 1:
                    dve.wait_ge(z_lo, b)
                nc.vector.tensor_tensor(small[:, :], scale_bank[b][:, :],
                                        yT[:, b % 2].rearrange("p c t -> p (c t)"), ALU.mult
                                        ).then_inc(z_ready, 1)

            def z_rest(b):
                dve.wait_ge(z_hi, b + 1)
                subtract(z_pair[:, b % 2, LO], small[:, :].rearrange("p (c t) -> p c t", c=HC),
                         z_pair[:, b % 2, HI]).then_inc(z_lo, 1)

            def gate_max(b):
                dve.wait_ge(logit_ready, b + 1)
                if b >= 1:
                    dve.wait_ge(gexp_ready, b)
                nc.vector.tensor_reduce(gmax[:, :], route_bank[b][:, 0:E], AX.X, ALU.max, negate=True
                                        ).then_inc(gmax_ready, 1)

            def gate_route(b):
                dve.wait_ge(gexp_ready, b + 1)
                nc.vector.reciprocal(grec[:, :], gsum[:, :]).then_inc(grec_ready, 1)
                dve.wait_ge(grec_ready, b + 1)
                if b >= 1:
                    dve.wait_ge(route_ready, b)
                nc.vector.tensor_scalar(route[:, :], gexp[:, :], grec[:, :], None, ALU.mult
                                        ).then_inc(route_split, 1)
                dve.wait_ge(route_split, 3 * b + 1)
                if b >= 1:
                    dve.wait_ge(routet_ready, b)
                rounded = route3[:, :].bitcast(f32r)
                for r in range(2):
                    nc.vector.tensor_copy(rounded[:, 32 * r:32 * r + E], route[:, :]
                                          ).then_inc(route_split, 1)
                dve.wait_ge(route_split, 3 * b + 3)
                subtract(rounded[:, 64:64 + E], route[:, :], route3[:, 0:E]
                         ).then_inc(route_ready, 1)

            def ffn_scale(b):
                dve.wait_ge(ffn_ready, b + 1)
                dve.wait_ge(oscale_copied, b + 1)
                nc.vector.tensor_tensor(oscale[:, b % OS], prod_bank[b][:, :], oscale[:, b % OS], ALU.mult
                                        ).then_inc(scaled_ready, 1)

            def last_out(b):
                dve.wait_ge(scaled_ready, b + 1)
                dve.wait_ge(bias_added, b + 1)
                nc.vector.tensor_tensor(acc[:, b], acc[:, b], oscale[:, b % OS], ALU.add
                                        ).then_inc(last_out_ready, 1)

            def group(g, last):
                for qd in range(QUADS):
                    final = last and qd == QUADS - 1
                    nxt = (g, qd + 1) if qd + 1 < QUADS else (g + 1, 0)
                    q_rest(g, qd, 2)
                    if final:
                        sgn(0)
                    q_rest(g, qd, 3)
                    row_max(g, qd, 0, 0)
                    if final:
                        sgn(1)
                    q_rest(g, qd, 4)
                    row_max(g, qd, 0, 1)
                    row_recip(g, qd, 0, 0)
                    row_recip(g, qd, 0, 1)
                    if final:
                        sgn(2)
                    q_rest(g, qd, 5)
                    if final:
                        sgn(3)
                        dve.wait_ge(route3_zeroed, 1)
                    q_rest(g, qd, 6)
                    for t in range(B):
                        if t + 1 < B:
                            row_max(g, qd, t + 1, 0)
                        if final and t >= 3:
                            gate_max(t - 3)
                        pt_rest(g, qd, t, 0)
                        if final and t >= 3:
                            gate_route(t - 3)
                        if t + 1 < B:
                            row_recip(g, qd, t + 1, 0)
                            row_max(g, qd, t + 1, 1)
                        pt_rest(g, qd, t, 1)
                        if t + 1 < B:
                            row_recip(g, qd, t + 1, 1)
                        if t == 0:
                            q_rest(g, qd, UNITS - 1)
                        if t == B - 1 and not final:
                            q_rest(*nxt, 0)
                        if t >= 1:
                            accumulate(g, qd, t - 1)
                            if final:
                                ffn_stats(t - 1)
                        if final and t >= 3:
                            z_make(t - 3)
                            z_rest(t - 3)
                        o_rest(g, qd, t)
                        if final and t >= 1:
                            ffn_norm(t - 1)
                        if final and t >= 4:
                            ffn_scale(t - 4)
                    if not final:
                        q_rest(*nxt, 1)
                    accumulate(g, qd, B - 1)

            q_rest(0, 0, 0)
            q_rest(0, 0, 1)
            with dve.Fori(0, G - 1) as g:
                group(g, False)
            group(G - 1, True)
            ffn_stats(B - 1)
            gate_max(B - 3)
            gate_route(B - 3)
            ffn_norm(B - 1)
            z_make(B - 3)
            gate_max(B - 2)
            z_rest(B - 3)
            gate_route(B - 2)
            ffn_scale(B - 4)
            z_make(B - 2)
            gate_max(B - 1)
            z_rest(B - 2)
            gate_route(B - 1)
            ffn_scale(B - 3)
            z_make(B - 1)
            z_rest(B - 1)
            ffn_scale(B - 2)
            ffn_scale(B - 1)
            last_out(B - 1)

        @block.tensor
        def _(pe):
            open_loop(pe, *s_ready, *pt_ready, av_ready, wo_ready)

            def product(dst, left, right, chunks, landing=None):
                n = 0
                for i, (a, b) in enumerate(TERMS):
                    for c in range(chunks):
                        if landing and i < 2:
                            pe.wait_ge(landing[b], c + 1)
                        last = nc.tensor.matmul(dst, left(a, c), right(b, c), start=(n == 0),
                                                stop=(n == 3 * chunks - 1))
                        n += 1
                return last

            def xt_transpose(b):
                pe.wait_ge(y_ready, b + 1)
                pe.wait_ge(xt_lo, b)
                for c in range(HC):
                    last = nc.tensor.transpose(t_bank[0][:, c * T:(c + 1) * T],
                                               y[:, b % 2, c * P:(c + 1) * P], ident[:, :])
                last.then_inc(xt_ready, 1)

            def ct_transpose(b):
                pe.wait_ge(c_in[b], 16)
                pe.wait_ge(ct_lo, b)
                for c in range(HC):
                    last = nc.tensor.transpose(t_bank[1][:, c * T:(c + 1) * T],
                                               craw[:, b, c * P:(c + 1) * P], ident[:, :])
                last.then_inc(ct_ready, 1)

            pe.wait_ge(const_ready, 2)
            ct_transpose(0)
            xt_transpose(0)
            for b in range(B):
                for kc, (src, lo_sem) in enumerate(((cT, ct_lo), (xT, xt_lo))):
                    n = 2 * b + kc
                    pe.wait_ge(lo_sem, b + 1)
                    if n >= 2:
                        pe.wait_ge(proj_lo, n - 1)
                    product(proj_bank[n % 2][:, :],
                            lambda s, c: src[:, s, c, b * T:(b + 1) * T],
                            lambda s, c: wv_pair[:, s, c, :], HC,
                            (wv_hi, wv_lo) if n == 0 else None).then_inc(proj_ready, 1)
                    if b + 1 < B:
                        (ct_transpose, xt_transpose)[kc](b + 1)
            pe.wait_ge(gate_in, 16)
            pe.wait_ge(xt_lo, B)
            for c in range(HC):
                last = nc.tensor.matmul(t_bank[0][:, c * E:(c + 1) * E],
                                        small[0:E, c * P:(c + 1) * P], ident[0:E, 0:E],
                                        start=True, stop=True)
            last.then_inc(gatet_ready, 1)
            pe.wait_ge(wk_lo, HC)
            for u in range(G * NHALF):
                g, half = divmod(u, NHALF)
                for kc, src in enumerate((cT, xT)):
                    n = 2 * B + 2 * u + kc
                    pe.wait_ge(proj_lo, n - 1)
                    product(proj_bank[n % 2][:, :],
                            lambda s, c: wk_pair[:, s, c, g * P:(g + 1) * P],
                            lambda s, c: src[:, s, c, half * 512:(half + 1) * 512], HC
                            ).then_inc(proj_ready, 1)

            def q_unit(g, qd, u):
                half, h = divmod(u, QH)
                if u == 0:
                    pe.wait_ge(wq_lo, count(g, HC, qd, HC))
                pe.wait_ge(proj_lo, count(g, UNITS, qd, PRE_UNITS + u - 1))
                product(proj_bank[u % 2][:, :],
                        lambda s, c: wq_pair[:, s, c, h * P:(h + 1) * P],
                        lambda s, c: xT[:, s, c, half * 512:(half + 1) * 512], HC
                        ).then_inc(proj_ready, 1)

            def scores(g, qd, t, p):
                if t % HALF == 0:
                    pe.wait_ge(proj_lo, count(g, UNITS, qd, PRE_UNITS + QH * (t // HALF) + 2 * p + 2))
                if qd == 0 and p == 0:
                    pe.wait_ge(k_in[t], 16 * (g + 1))
                pe.wait_ge(exp_ready[p], steps(g, qd, t))
                for j in range(2):
                    h = 2 * p + j
                    last = product(s_bank[p][:, j * KEYS:(j + 1) * KEYS],
                                   lambda s, c: qT[:, s, h, t * T:(t + 1) * T],
                                   lambda s, c: kg[:, t, s, :], 1)
                last.then_inc(s_ready[p], 1)

            def transposes(g, qd, t, p):
                pe.wait_ge(prob_ready[p], steps(g, qd, t + 1))
                pe.wait_ge(pt_lo[p], steps(g, qd, t))
                for kc in range(KC):
                    for j in range(2):
                        at = (2 * kc + j) * T
                        last = nc.tensor.transpose(t_bank[p][:, at:at + T],
                                                   prob[:, p, j, kc * P:(kc + 1) * P], ident[:, :])
                last.then_inc(pt_ready[p], 1)

            def attend(g, qd, t):
                if qd == 0:
                    pe.wait_ge(v_in[t], 16 * (g + 1))
                pe.wait_ge(o_lo, steps(g, qd, t))
                n = 0
                pe.wait_ge(pt_hi[1], steps(g, qd, t + 1))
                pe.wait_ge(pt_hi[0], steps(g, qd, t + 1))
                for vs, ps in ((HI, HI), (LO, HI), (HI, LO)):
                    if ps == LO:
                        pe.wait_ge(pt_lo[0], steps(g, qd, t + 1))
                        pe.wait_ge(pt_lo[1], steps(g, qd, t + 1))
                    for kc in range(KC):
                        last = nc.tensor.matmul(av_bank[:, :], vg[:, t, vs, kc, :],
                                                pT[:, ps, kc].rearrange("p h t -> p (h t)"),
                                                start=(n == 0), stop=(n == 3 * KC - 1))
                        n += 1
                last.then_inc(av_ready, 1)

            def project_out(g, qd, t, heads):
                if heads[0] == 0:
                    if t == 0:
                        pe.wait_ge(wo_lo, count(g, QH, qd, QH))
                    pe.wait_ge(acc_ready, steps(g, qd, t))
                    pe.wait_ge(o_hi, steps(g, qd, t + 1))
                for s, w in TERMS:
                    if s == LO and heads[0] == 0:
                        pe.wait_ge(o_lo, steps(g, qd, t + 1))
                    for h in heads:
                        last = nc.tensor.matmul(
                            wo_bank[:, :], oT[:, s, h, :], wo_pair[:, w, h, :],
                            start=((s, w) == TERMS[0] and h == 0),
                            stop=((s, w) == TERMS[-1] and h == QH - 1))
                if heads[-1] == QH - 1:
                    last.then_inc(wo_ready, 1)

            def sgn_transpose(c):
                pe.wait_ge(sgn_ready, HC)
                if c >= 2:
                    pe.wait_ge(sgnt_copied, c - 1)
                else:
                    pe.wait_ge(proj_lo, count(G - 1, UNITS, QUADS - 1, PRE_UNITS + UNITS))
                for r in range(HC):
                    last = nc.tensor.transpose(proj_bank[c % 2][:, r * P:(r + 1) * P],
                                               raw_a[:, r, c * P:(c + 1) * P], ident[:, :])
                last.then_inc(sgnt_ready, 1)

            def y_transpose(b):
                pe.wait_ge(y_ready, B + b + 1)
                if b == 0:
                    pe.wait_ge(sgnt_copied, HC)
                elif b < B - 2:
                    pe.wait_ge(z_ready, b)
                else:
                    pe.wait_ge(pt_lo[b - (B - 2)], steps(G - 1, QUADS - 1, B))
                for c in range(HC):
                    last = nc.tensor.transpose(scale_bank[b][:, c * T:(c + 1) * T],
                                               y[:, b % 2, c * P:(c + 1) * P], ident[:, :])
                last.then_inc(yt_ready, 1)

            def logits(b):
                pe.wait_ge(yt_copied, b + 1)
                if b >= B - 2:
                    pe.wait_ge(exp_ready[b - (B - 2)], steps(G - 1, QUADS - 1, B))
                elif b == B - 3:
                    pe.wait_ge(scaled_ready, B - 4)
                elif b >= 2:
                    pe.wait_ge(scaled_ready, b - 1)
                for c in range(HC):
                    last = nc.tensor.matmul(route_bank[b][:, 0:E], yT[:, b % 2, c, :],
                                            gateT[:, c, :], start=(c == 0), stop=(c == HC - 1))
                last.then_inc(logit_ready, 1)

            def route_transpose(b):
                pe.wait_ge(route_ready, b + 1)
                nc.tensor.transpose(route_bank[b][:, 0:T], route3[:, :], ident[:, :]
                                    ).then_inc(routet_ready, 1)

            def channel_scales(b):
                pe.wait_ge(routet_copied, b + 1)
                for c in range(HC):
                    last = nc.tensor.matmul(scale_bank[b][:, c * T:(c + 1) * T],
                                            scales[:, 0, c * P:(c + 1) * P], routeT[:, :],
                                            start=True, stop=True)
                last.then_inc(iscale_ready, 1)
                nc.tensor.matmul(route_bank[b][:, :], routeT[:, :], scales[:, 1, :], start=True,
                                 stop=True).then_inc(oscale_ready, 1)

            def ffn_product(b):
                if b < B - 4:
                    pe.wait_ge(oscale_copied, b + 2)
                elif b == B - 4:
                    pe.wait_ge(o_lo, steps(G - 1, QUADS - 1, B))
                elif b == B - 3:
                    pe.wait_ge(acc_ready, steps(G - 1, QUADS - 1, B))
                elif b == B - 2:
                    pe.wait_ge(oscale_copied, B - 2)
                else:
                    pe.wait_ge(z_ready, B - 2)
                for s in (HI, LO):
                    pe.wait_ge((z_hi, z_lo)[s], b + 1)
                    for c in range(HC):
                        last = nc.tensor.matmul(prod_bank[b][:, :], z_pair[:, b % 2, s, c, :],
                                                sgnT[:, c, :], start=(s == HI and c == 0),
                                                stop=(s == LO and c == HC - 1))
                last.then_inc(ffn_ready, 1)

            def group(g, last):
                for qd in range(QUADS):
                    final = last and qd == QUADS - 1
                    nxt = (g, qd + 1) if qd + 1 < QUADS else (g + 1, 0)
                    q_unit(g, qd, 2)
                    q_unit(g, qd, 3)
                    scores(g, qd, 0, 0)
                    q_unit(g, qd, 4)
                    scores(g, qd, 0, 1)
                    q_unit(g, qd, 5)
                    q_unit(g, qd, 6)
                    for t in range(B):
                        if t + 1 < B:
                            scores(g, qd, t + 1, 0)
                        if final and t >= 3:
                            logits(t - 3)
                        transposes(g, qd, t, 0)
                        if 1 <= t < B - 1:
                            project_out(g, qd, t - 1, (0, 1))
                        if final and t == 1:
                            sgn_transpose(0)
                            sgn_transpose(1)
                        if t + 1 < B:
                            scores(g, qd, t + 1, 1)
                        transposes(g, qd, t, 1)
                        if final and t >= 3:
                            route_transpose(t - 3)
                        if t == 0:
                            q_unit(g, qd, UNITS - 1)
                        elif t < B - 1:
                            project_out(g, qd, t - 1, (2, 3))
                        else:
                            if not final:
                                q_unit(*nxt, 0)
                            project_out(g, qd, t - 1, range(QH))
                        if final and t == 1:
                            sgn_transpose(2)
                            sgn_transpose(3)
                        if final and t >= 3:
                            channel_scales(t - 3)
                        attend(g, qd, t)
                        if final and t >= 2:
                            y_transpose(t - 2)
                        if final and t >= 4:
                            ffn_product(t - 4)
                    if not final:
                        q_unit(*nxt, 1)
                    project_out(g, qd, B - 1, range(QH))

            q_unit(0, 0, 0)
            q_unit(0, 0, 1)
            pe.wait_ge(gatet_copied, 1)
            with pe.Fori(0, G - 1) as g:
                group(g, False)
            pe.wait_ge(scales_ready, 1)
            group(G - 1, True)
            logits(B - 3)
            y_transpose(B - 2)
            route_transpose(B - 3)
            ffn_product(B - 4)
            channel_scales(B - 3)
            logits(B - 2)
            y_transpose(B - 1)
            route_transpose(B - 2)
            channel_scales(B - 2)
            ffn_product(B - 3)
            logits(B - 1)
            route_transpose(B - 1)
            ffn_product(B - 2)
            channel_scales(B - 1)
            ffn_product(B - 1)


_INS = ["x", "ctx_4096", "L0_xattn_Wq", "L0_xattn_Wk", "L0_xattn_Wv", "L0_xattn_Wo", "L0_ffn_weight",
        "L0_ffn_bias", "L0_ffn_gate_w", "L0_ffn_in_channel_scale", "L0_ffn_out_channel_scale"]


def kernel(**inputs):
    import numpy as np
    import concourse.bacc as bacc
    from concourse.bass_utils import run_bass_kernel_spmd

    nc = bacc.Bacc("TRN2", target_bir_lowering=False, num_devices=1)
    arrays, args = {}, []
    for name in _INS:
        a = np.ascontiguousarray(inputs[name])
        arrays[f"in_{name}"] = a
        args.append(nc.dram_tensor(f"in_{name}", a.shape, mybir.dt.from_np(a.dtype),
                                   kind="ExternalInput").ap())
    args.append(nc.dram_tensor("out_y", arrays["in_x"].shape, mybir.dt.float32,
                               kind="ExternalOutput").ap())
    xattn_ffn(nc, *args)
    result = run_bass_kernel_spmd(nc, [arrays], core_ids=[0])
    return result.results[0]["out_y"]
```
